# Optimizing a Trainium2 kernel written in Bass

```python
import numpy as np
import jax
import jax.numpy as jnp

def _softmax(x, axis=-1):
    return jax.nn.softmax(x, axis=axis)

def _gelu(x):
    return jax.nn.gelu(x, approximate=True)

def _silu(x):
    return jax.nn.silu(x)

def _sigmoid(x):
    return jax.nn.sigmoid(x)

def _layernorm(x, axis=-1, eps=1e-05):
    m = jnp.mean(x, axis=axis, keepdims=True)
    v = jnp.var(x, axis=axis, keepdims=True)
    return (x - m) / jnp.sqrt(v + eps)

def _scatter_add(tgt, idx, src, axis=0):
    return tgt.at[idx].add(src)

def _segment_sum(src, seg, n):
    return jax.ops.segment_sum(src, seg, n)
kernel_name = 'mk_conv_preact_d2_conv_nchw64_r2_425499'

def setup_inputs(seed: int=0):
    np.random.seed(seed)
    _w = jnp.asarray

    def _rec_inputs():
        import jax
        import jax.numpy as jnp
        _gk = jax.random.key(seed)
        x = -7.109e-05 + 0.9999 * jax.random.normal(jax.random.fold_in(_gk, 1), (16, 32, 128, 128), jnp.float32)
        return x
    x = _rec_inputs()

    def _L0_conv_setup():
        import jax, jax.numpy as jnp
        import numpy as np
        TEMPERATURE = 30.0
        BN_EPS = 1e-05
        PAD = 1
        key = jax.random.key(seed)
        ks = jax.random.split(key, 6)
        B, C, H, W = (16, 32, 128, 128)
        HID, K, KS = (17, 4, 3)
        OUT = 32
        return {'x': jax.random.normal(ks[0], (B, C, H, W), jnp.float32), 'att_w1': jax.random.normal(ks[1], (HID, C), jnp.float32) * 0.1, 'bn_gamma': jnp.ones((HID,), jnp.float32), 'bn_beta': jnp.zeros((HID,), jnp.float32), 'att_w2': jax.random.normal(ks[2], (K, HID), jnp.float32) * 0.1, 'weight': jax.random.normal(ks[3], (K, C, 1, KS, KS), jnp.float32) * 0.1, 'conv1_w': jax.random.normal(ks[4], (OUT, C), jnp.float32) * 0.1, 'conv1_b': jnp.zeros((OUT,), jnp.float32)}
    _L0_conv_all = _L0_conv_setup()
    _L0_conv_in = {k: v for k, v in _L0_conv_all.items() if k in ('att_w1', 'bn_gamma', 'bn_beta', 'att_w2', 'weight', 'conv1_w', 'conv1_b')}
    del _L0_conv_all

    def _L1_conv_setup():
        import jax, jax.numpy as jnp
        import numpy as np
        from jax import lax
        DIM = 32
        B, H, W = (4, 128, 128)
        key = jax.random.key(seed)
        ks = jax.random.split(key, 6)
        d = DIM
        x = jax.random.normal(ks[0], (B, d, H, W), dtype=jnp.float32)
        w_hidden = jax.random.normal(ks[1], (6 * d, d), dtype=jnp.float32) * 0.05
        w_dw = jax.random.normal(ks[2], (6 * d, 1, 3, 3), dtype=jnp.float32) * 0.05
        norm_w = jnp.ones((2 * d,), dtype=jnp.float32)
        norm_b = jnp.zeros((2 * d,), dtype=jnp.float32)
        w_out = jax.random.normal(ks[3], (d, 2 * d), dtype=jnp.float32) * 0.05
        return {'x': x, 'w_hidden': w_hidden, 'w_dw': w_dw, 'norm_w': norm_w, 'norm_b': norm_b, 'w_out': w_out, 'patch_size': 8}
    _L1_conv_all = _L1_conv_setup()
    _L1_conv_in = {k: v for k, v in _L1_conv_all.items() if k in ('w_hidden', 'w_dw', 'norm_w', 'norm_b', 'w_out')}
    del _L1_conv_all
    return {'x': x, 'L0_conv_att_w1': _L0_conv_in['att_w1'], 'L0_conv_bn_gamma': _L0_conv_in['bn_gamma'], 'L0_conv_bn_beta': _L0_conv_in['bn_beta'], 'L0_conv_att_w2': _L0_conv_in['att_w2'], 'L0_conv_weight': _L0_conv_in['weight'], 'L0_conv_conv1_w': _L0_conv_in['conv1_w'], 'L0_conv_conv1_b': _L0_conv_in['conv1_b'], 'L1_conv_w_hidden': _L1_conv_in['w_hidden'], 'L1_conv_w_dw': _L1_conv_in['w_dw'], 'L1_conv_norm_w': _L1_conv_in['norm_w'], 'L1_conv_norm_b': _L1_conv_in['norm_b'], 'L1_conv_w_out': _L1_conv_in['w_out']}

def reference(x, L0_conv_att_w1, L0_conv_bn_gamma, L0_conv_bn_beta, L0_conv_att_w2, L0_conv_weight, L0_conv_conv1_w, L0_conv_conv1_b, L1_conv_w_hidden, L1_conv_w_dw, L1_conv_norm_w, L1_conv_norm_b, L1_conv_w_out):
    import jax
    import jax.numpy as jnp

    def _L0_conv_ref(x, att_w1, bn_gamma, bn_beta, att_w2, weight, conv1_w, conv1_b):
        import jax, jax.numpy as jnp
        import numpy as np
        TEMPERATURE = 30.0
        BN_EPS = 1e-05
        PAD = 1
        B, C, H, W = x.shape
        K = weight.shape[0]
        pooled = x.mean(axis=(2, 3))
        a = pooled @ att_w1.T
        a = a * (bn_gamma / jnp.sqrt(1.0 + BN_EPS)) + bn_beta
        a = jax.nn.relu(a)
        logits = a @ att_w2.T
        softmax_att = jax.nn.softmax(logits / TEMPERATURE, axis=1)
        sig_att = jax.nn.sigmoid(pooled)
        xs = x * sig_att[:, :, None, None]
        agg_w = jnp.einsum('bk,kcij->bcij', softmax_att, weight[:, :, 0])

        def dwconv(xb, wb):
            return jax.lax.conv_general_dilated(xb[None], wb[:, None], window_strides=(1, 1), padding=((PAD, PAD), (PAD, PAD)), feature_group_count=C, dimension_numbers=('NCHW', 'OIHW', 'NCHW'))[0]
        out = jax.vmap(dwconv)(xs, agg_w)
        out_f = jnp.einsum('bchw,oc->bohw', out, conv1_w) + conv1_b[None, :, None, None]
        return out_f

    def _L1_conv_ref(x, w_hidden, w_dw, norm_w, norm_b, w_out, patch_size):
        import jax, jax.numpy as jnp
        import numpy as np
        from jax import lax
        DIM = 32
        B, H, W = (4, 128, 128)
        p = patch_size
        b, c, h, w = x.shape
        hidden = jnp.einsum('oc,bchw->bohw', w_hidden, x)
        hidden = lax.conv_general_dilated(hidden, w_dw, window_strides=(1, 1), padding='SAME', dimension_numbers=('NCHW', 'OIHW', 'NCHW'), feature_group_count=w_dw.shape[0])
        q, k, v = jnp.split(hidden, 3, axis=1)
        c2 = 2 * c

        def to_patch(t):
            return t.reshape(b, c2, h // p, p, w // p, p).transpose(0, 1, 2, 4, 3, 5)
        q_fft = jnp.fft.rfft2(to_patch(q).astype(jnp.float32))
        k_fft = jnp.fft.rfft2(to_patch(k).astype(jnp.float32))
        out = jnp.fft.irfft2(q_fft * k_fft, s=(p, p))
        out = out.transpose(0, 1, 2, 4, 3, 5).reshape(b, c2, h, w)
        mu = out.mean(axis=1, keepdims=True)
        var = out.var(axis=1, keepdims=True)
        out_norm = (out - mu) / jnp.sqrt(var + 1e-05)
        out_norm = out_norm * norm_w[None, :, None, None] + norm_b[None, :, None, None]
        gated = v * out_norm
        return jnp.einsum('oc,bchw->bohw', w_out, gated)

    def _gn(v, G=32, eps=1e-05):
        B_, C_, H_, W_ = v.shape
        g = v.reshape(B_, G, C_ // G, H_, W_)
        m = jnp.mean(g, axis=(2, 3, 4), keepdims=True)
        s = jnp.var(g, axis=(2, 3, 4), keepdims=True)
        return ((g - m) / jnp.sqrt(s + eps)).reshape(v.shape)

    def _ln_c(v, eps=1e-06):
        m = jnp.mean(v, axis=1, keepdims=True)
        s = jnp.var(v, axis=1, keepdims=True)
        return (v - m) / jnp.sqrt(s + eps)

    def _ln_t(v, eps=1e-05):
        m = jnp.mean(v, axis=-1, keepdims=True)
        s = jnp.var(v, axis=-1, keepdims=True)
        return (v - m) / jnp.sqrt(s + eps)

    def _to_tokens(v):
        B_, C_, H_, W_ = v.shape
        return v.reshape(B_, C_, H_ * W_).transpose(0, 2, 1)

    def _from_tokens(t, like):
        B_, C_, H_, W_ = like.shape
        return t.transpose(0, 2, 1).reshape(B_, C_, H_, W_)
    x = x + _L0_conv_ref(_gn(x), L0_conv_att_w1, L0_conv_bn_gamma, L0_conv_bn_beta, L0_conv_att_w2, L0_conv_weight, L0_conv_conv1_w, L0_conv_conv1_b)
    x = x + _L1_conv_ref(_gn(x), L1_conv_w_hidden, L1_conv_w_dw, L1_conv_norm_w, L1_conv_norm_b, L1_conv_w_out, 8)
    return x

_drawn_inputs = setup_inputs


def setup_inputs(seed=0):
    import zlib

    import numpy as np

    out = dict(_drawn_inputs(seed))
    spreads = {'L0_conv_bn_gamma': (1.0, 0.2),
     'L0_conv_bn_beta': (0.0, 2.0),
     'L0_conv_conv1_b': (0.0, 0.1),
     'L1_conv_norm_w': (1.0, 0.6),
     'L1_conv_norm_b': (0.0, 0.8)}
    factors = {'L0_conv_att_w2': 64.0,
     'L1_conv_w_hidden': 3.49,
     'L1_conv_w_dw': 3.549,
     'L1_conv_w_out': 3.587}
    for name, (base, spread) in spreads.items():
        noise = np.random.default_rng([zlib.crc32(name.encode()), seed]).standard_normal(out[name].shape)
        drawn = base * np.exp(spread * noise) if base else spread * noise
        out[name] = jnp.asarray(drawn.astype(out[name].dtype))
    for name, factor in factors.items():
        out[name] = (out[name] * factor).astype(out[name].dtype)
    return out
```

```python
from contextlib import ExitStack

import numpy as np

import concourse.bass as bass
from concourse import mybir

EPS = 1e-5
TEMPERATURE = 30.0
X_SCALE = 256.0
TINY = 1e-30


def constants():
    p = np.arange(128)
    same_channel = (p[:, None] % 32 == p[None, :] % 32).astype(np.float32)
    out = {"identity": np.eye(128, dtype=np.float32), "quarter_mean": same_channel / 4,
           "image_mean": same_channel / (4 * 4096)}
    group = np.zeros((128, 32), np.float32)
    for g in range(3):
        group[32 * g:32 * g + 32, g] = 1
    out["tap_group"] = group
    support = np.zeros((32, 130, 128), np.float32)
    support[0, 1:129, 1:] = 1
    support[1, 1:129, :] = 1
    support[2, 1:129, :127] = 1
    support[3] = 1
    out["support"] = support.reshape(32, 130 * 128)
    u, v = np.meshgrid(np.arange(8), np.arange(8), indexing="ij")
    u, v = u.ravel(), v.ravel()
    spectra = np.zeros((9, 3, 64, 10, 10), np.float64)
    for dy in range(3):
        for dx in range(3):
            for y in range(8):
                for x in range(8):
                    a = 2 * np.pi * ((u * y + v * x) % 8) / 8
                    spectra[3 * dy + dx, :, :, y + dy, x + dx] = [np.cos(a), np.sin(a), np.cos(a) + np.sin(a)]
    out["spectra"] = spectra.reshape(9, 192 * 100).astype(np.float32)
    a = 2 * np.pi * ((u[:, None] * u[None, :] + v[:, None] * v[None, :]) % 8) / 8
    out["inverse"] = (np.concatenate([np.cos(a) + np.sin(a), np.sin(a) - np.cos(a)]) / 64).astype(np.float32)
    return out


def build(nc, t, out):
    f32, f16 = mybir.dt.float32, mybir.dt.float16
    ALU, ACT, X_AXIS = mybir.AluOpType, mybir.ActivationFunctionType, mybir.AxisListType.X
    x = t["x"]
    NB, C, H, W = x.shape
    PIX = H * W
    Q = 4
    QPIX = PIX // Q
    NCH = QPIX // 512
    WP = W + 2
    HALF = H // 2 + 2
    WIN = 100
    LAST = 2 * NB - 1

    def dram(name, shape, dt):
        return nc.dram_tensor(name, shape, dt, kind="Internal").ap()

    x2_d = dram("x2_d", [NB, C, PIX], f32)
    xn_d = dram("xn_d", [NB, 2, C, H + 2, WP], f16)

    ctx = ExitStack()
    with ctx:
        def sb(name, cols, dt=f32, rows=128):
            return ctx.enter_context(nc.sbuf_tensor(name, [rows, cols], dt))[:, :]

        banks = [ctx.enter_context(nc.psum_tensor(f"bank{i}", [128, 512], f32))[:, :] for i in range(8)]
        def semaphore(name):
            return ctx.enter_context(nc.semaphore(name))

        def positive(value):
            return not isinstance(value, int) or value > 0

        s_small_in = semaphore("small_in")
        s_support_in = semaphore("support_in")
        s_x3_in = [semaphore(f"x3_in{s}") for s in range(2)]
        s_xq_in = [semaphore(f"xq_in{s}") for s in range(2)]
        s_x2_out = [semaphore(f"x2_out{s}") for s in range(2)]
        s_xn_out = semaphore("xn_out")
        s_spectra_in = semaphore("spectra_in")
        s_xs_in = [semaphore(f"xs_in{s}") for s in range(2)]
        s_res_in = semaphore("res_in")
        s_out_stored = semaphore("out_stored")
        s_x3_zero = semaphore("x3_zero")
        s_pads_zero = semaphore("pads_zero")
        s_pool_consts = semaphore("pool_consts")
        s_win_room = semaphore("win_room")
        s_prep = semaphore("prep")
        s_prep_qk = semaphore("prep_qk")
        s_prep_v = semaphore("prep_v")
        s_v_consts = semaphore("v_consts")
        s_qk_t = semaphore("qk_t")
        s_v_t = semaphore("v_t")
        s_hidden_hi = semaphore("hidden_hi")
        s_dw_t = semaphore("dw_t")
        s_v_hi = semaphore("v_hi")
        s_low_parts = semaphore("low_parts")
        s_g_mm = semaphore("g_mm")
        s_g_ready = semaphore("g_ready")
        s_st = {k: semaphore(f"st{k}") for k in (1, 2)}
        s_mv = {k: semaphore(f"mv{k}") for k in (1, 2)}
        s_mean_mm = {k: semaphore(f"mean_mm{k}") for k in (1, 2)}
        s_dev = {k: semaphore(f"dev{k}") for k in (1, 2)}
        s_varq = {k: semaphore(f"varq{k}") for k in (1, 2)}
        s_var_mm = {k: semaphore(f"var_mm{k}") for k in (1, 2)}
        s_ve = {k: semaphore(f"ve{k}") for k in (1, 2)}
        s_rstd = {k: semaphore(f"rstd{k}") for k in (1, 2)}
        s_shift1 = semaphore("shift1")
        s_xnsum = semaphore("xnsum")
        s_pooled_mm = semaphore("pooled_mm")
        s_pooled = semaphore("pooled")
        s_hid_mm = semaphore("hid_mm")
        s_hid = semaphore("hid")
        s_hid_relu = semaphore("hid_relu")
        s_logit_mm = semaphore("logit_mm")
        s_neg_max = semaphore("neg_max")
        s_neg_max_t = semaphore("neg_max_t")
        s_gate_exp = semaphore("gate_exp")
        s_gate_den = semaphore("gate_den")
        s_gate = semaphore("gate")
        s_chan_scale = semaphore("chan_scale")
        s_exps = semaphore("exps")
        s_exp_inv = semaphore("exp_inv")
        s_att = semaphore("att")
        s_att_mm = semaphore("att_mm")
        s_att_all = semaphore("att_all")
        s_agg = semaphore("agg")
        s_mean_w = semaphore("mean_w")
        s_corr_mm = semaphore("corr_mm")
        s_conv_w = semaphore("conv_w")
        s_edges = semaphore("edges")
        s_conv_mm = semaphore("conv_mm")
        s_x2_ready = semaphore("x2_ready")
        s_scale2 = semaphore("scale2")
        s_shift2 = semaphore("shift2")
        s_xh_ready = semaphore("xh_ready")
        s_xnf_ready = semaphore("xnf_ready")
        s_xl_ready = semaphore("xl_ready")
        s_win_ready = semaphore("win_ready")
        s_hidden_mm = semaphore("hidden_mm")
        s_h_ready = semaphore("h_ready")
        s_q_mm = semaphore("q_mm")
        s_q_copied = semaphore("q_copied")
        s_k_mm = semaphore("k_mm")
        s_prod_ready = semaphore("prod_ready")
        s_inverse_mm = semaphore("inverse_mm")
        s_y_ready = semaphore("y_ready")
        s_sums = semaphore("sums")
        s_neg_mu = semaphore("neg_mu")
        s_y_centred = semaphore("y_centred")
        s_squared = semaphore("squared")
        s_sq_sums = semaphore("sq_sums")
        s_var_eps = semaphore("var_eps")
        s_root = semaphore("root")
        s_y_norm = semaphore("y_norm")
        s_turned = semaphore("turned")
        s_t_copied = semaphore("t_copied")
        s_v_mm = semaphore("v_mm")
        s_gated = semaphore("gated")
        s_project_mm = semaphore("project_mm")
        s_res_done = semaphore("res_done")

        def at(ap, offset, *dims):
            return bass.AP(tensor=ap.tensor, offset=ap.offset + offset, ap=[ap.ap[0]] + [list(d) for d in dims])

        WORDS = 53200
        arena = sb("arena", WORDS)
        top = [0]

        def take(cols, dt=f32):
            words = cols if dt == f32 else (cols + 1) // 2
            a = arena[:, top[0]:top[0] + words]
            top[0] += words
            assert top[0] <= WORDS, top[0]
            return a if dt == f32 else a.bitcast(dt)

        small = {n: take(t[n].shape[1]) for n in ("identity", "inverse", "w_out")}
        ident = small["identity"]
        hidden_w = take(128, f16)
        v_w = take(9 * 64, f16)
        powers = take(16)
        tiny = {n: take(c) for n, c in (("v_scale", 1), ("v_shift", 1), ("sums", 16), ("neg_mu", 16),
                                        ("sq_sums", 16), ("var_eps", 16), ("rstd", 16))}
        phases = top[0]

        x3 = [take((H + 2) * W) for _ in range(2)]
        xq = [take(QPIX) for _ in range(2)]
        xnf = take(QPIX)
        xh, xl = take(QPIX // W * WP, f16), take(QPIX // W * WP, f16)
        prep_qk, prep_v = xnf[:, 0:128], xnf[:, 128:128 + 9 * 128]
        small |= {n: take(t[n].shape[1]) for n in
                  ("quarter_mean", "image_mean", "tap_group", "w1", "w2", "dyn_w", "conv1", "bias_row", "gamma", "beta",
                   "hidden_qk", "dw_qk", "hidden_v", "dw_v", "norm_w", "norm_b")}
        quarter_mean, image_mean = small["quarter_mean"], small["image_mean"]
        ones_row = take(128)
        conv_w = [take(96) for s in range(2)]
        mean_w = take(32)
        st1, st2 = take(6 * NCH), take(6 * NCH)
        tiny |= {n: take(c) for n, c in (
            ("mv1", 2), ("mean1", 1), ("dev1", 1), ("varq1", 1), ("ve1", 1), ("rstd1", 1), ("shift1", 1),
            ("mv2", 2), ("mean2", 1), ("dev2", 1), ("varq2", 1), ("ve2", 1), ("rstd2", 1), ("scale2", 1), ("shift2", 1),
            ("xnsum", 1), ("pooled", 1), ("hid", 1), ("hid_relu", 1), ("neg_max", 1), ("neg_max_t", 1), ("exps", 4),
            ("exp_sum", 1), ("exp_inv", 1), ("att", 4), ("att_all", 4), ("gate_exp", 1), ("gate_den", 1), ("gate", 1),
            ("chan_scale", 1), ("agg", 3), ("gammas", 1), ("qk_max", 1), ("qk_inv", 1), ("qk_back", 1),
            ("v_max", 1), ("v_inv", 1), ("d_max", 1), ("d_inv", 1), ("v_back", 1), ("dw_qk_s", 9), ("dw_v_n", 9))}
        phase_a_end = top[0]

        top[0] = phases
        hwin = take(128 * 128)
        Y = take(64 * 64)
        spec = arena[:, phases:phases + 192 * WIN]
        G = take(128 * 128)
        xs = [take(HALF * WP, f16) for _ in range(2)]
        q_sb = [take(512) for _ in range(2)]
        squares = arena[:, top[0] - 1024:top[0]]
        prod = [take(512) for _ in range(2)]
        gated = [take(512) for _ in range(2)]
        res = take(2048)
        win_at = top[0]
        win = [take(1632, f16) for _ in range(2)]
        dw_t = arena[:, max(win_at, phase_a_end):max(win_at, phase_a_end) + 128]
        assert max(win_at, phase_a_end) + 128 <= win_at + 800
        block = ctx.enter_context(nc.Block())

        def batch(pair, odd):
            return 2 * pair + odd, pair, odd

        @block.sync
        def _(sp):
            for name in small:
                rows = t[name].shape[0]
                sp.dma_start(small[name][0:rows, :], t[name]).then_inc(s_small_in, 16)

            def load_x3(b, n, s):
                flat = x[b].rearrange("c h w -> c (h w)")
                sp.dma_start(x3[s][0:32, W + 1:W + PIX], flat[:, 0:PIX - 1]).then_inc(s_x3_in[s], 16)
                sp.dma_start(x3[s][32:64, W:W + PIX], flat).then_inc(s_x3_in[s], 16)
                sp.dma_start(x3[s][64:96, W:W + PIX - 1], flat[:, 1:PIX]).then_inc(s_x3_in[s], 16)

            def load_xq(b, n, s):
                flat = x[b].rearrange("c h w -> c (h w)")
                for q in range(Q):
                    sp.dma_start(xq[s][32 * q:32 * q + 32, :], flat[:, q * QPIX:(q + 1) * QPIX]).then_inc(s_xq_in[s], 16)

            def store_a(b, n, s, more):
                sp.wait_ge(s_x2_ready, NCH * (b + 1))
                for q in range(Q):
                    sp.dma_start(x2_d[b, :, q * QPIX:(q + 1) * QPIX], xq[s][32 * q:32 * q + 32, :]).then_inc(s_x2_out[s], 16)
                if more is not None:
                    load_x3(*more)
                sp.wait_ge(s_xl_ready, b + 1)
                for part, buf in ((0, xh), (1, xl)):
                    for q in range(Q):
                        sp.dma_start(xn_d[b, part, :, 1 + q * (H // Q):1 + (q + 1) * (H // Q), :].rearrange("c h w -> c (h w)"),
                                     buf[32 * q:32 * q + 32, :]).then_inc(s_xn_out, 16)
                if more is not None:
                    sp.wait_ge(s_x2_out[s], 64 * (n + 1))
                    load_xq(*more)

            for s in range(2):
                load_xq(*batch(0, s))
                sp.wait_ge(s_x3_zero, 2)
                load_x3(*batch(0, s))
                sp.dma_start(x3[s][96:128, :], t["support"]).then_inc(s_support_in, 16)
            images = xn_d.rearrange("b g c h w -> (b g c) h w").rearrange("(p e) h w -> p e h w", p=128)
            sp.wait_ge(s_pads_zero, 2)
            for row in (0, H + 1):
                sp.dma_start(images[:, :, row, :], xh[:, 0:NB // 2 * WP].rearrange("p (e w) -> p e w", w=WP)).then_inc(s_xn_out, 16)
            with sp.Fori(0, NB // 2 - 1) as pair:
                for s in range(2):
                    store_a(*batch(pair, s), batch(pair + 1, s))
            for s in range(2):
                store_a(*batch(NB // 2 - 1, s), None)

            sp.wait_ge(s_x2_out[0], 64 * NB // 2)
            sp.wait_ge(s_x2_out[1], 64 * NB // 2)
            sp.wait_ge(s_xn_out, 128 * NB + 32)
            sp.wait_ge(s_xl_ready, NB)
            sp.dma_start(spec[0:9, :], t["spectra"]).then_inc(s_spectra_in, 16)

            def load_xs(b, half):
                for g in range(4):
                    src = xn_d[b, g % 2, :, half * (H // 2):half * (H // 2) + HALF, :].rearrange("c h w -> c (h w)")
                    sp.dma_start(xs[half][32 * g:32 * g + 32, :], src).then_inc(s_xs_in[half], 16)

            def image_rows(base, b, half, jr, s):
                first = (half * 8 + 2 * s + jr) * 8 * W
                return base[b, :, half * (PIX // 2):(half + 1) * (PIX // 2)].rearrange(
                    "c (l r) -> c l r", l=2)[:, :, first - half * (PIX // 2):first - half * (PIX // 2) + 8 * W]

            def load_res(b, half):
                for jr in range(2):
                    for s in range(2):
                        p0 = 64 * jr + 32 * s
                        sp.dma_start(res[p0:p0 + 32, :].rearrange("p (l r) -> p l r", l=2),
                                     image_rows(x2_d, b, half, jr, s)).then_inc(s_res_in, 16)

            def store_res(b, half):
                for jr in range(2):
                    for s in range(2):
                        p0 = 64 * jr + 32 * s
                        sp.dma_start(image_rows(out.rearrange("b c h w -> b c (h w)"), b, half, jr, s),
                                     res[p0:p0 + 32, :].rearrange("p (l r) -> p l r", l=2)).then_inc(s_out_stored, 16)

            load_xs(0, 0)
            load_xs(0, 1)
            load_res(0, 0)

            def unit_dma(u, prev, here, nxt):
                sp.wait_ge(s_v_mm, 8 * u)
                if nxt is not None:
                    load_xs(*nxt)
                sp.wait_ge(s_res_done, 4 * u)
                store_res(*prev)
                sp.wait_ge(s_out_stored, 64 * u)
                if here is not None:
                    load_res(*here)

            with sp.Fori(0, NB - 1) as b:
                unit_dma(2 * b + 1, (b, 0), (b, 1), (b + 1, 0))
                unit_dma(2 * b + 2, (b, 1), (b + 1, 0), (b + 1, 1))
            unit_dma(LAST, (NB - 1, 0), (NB - 1, 1), None)
            unit_dma(LAST + 1, (NB - 1, 1), None, None)
            sp.wait_ge(s_out_stored, 64 * 2 * NB)

        @block.gpsimd
        def _(pool):
            for s in range(2):
                pool.memset(x3[s][0:96, :], 0.0).then_inc(s_x3_zero, 1)
            pool.memset(xh.bitcast(f32), 0.0).then_inc(s_pads_zero, 1)
            pool.memset(xl.bitcast(f32), 0.0).then_inc(s_pads_zero, 1)
            pool.memset(powers, -0.5).then_inc(s_pool_consts, 1)
            pool.memset(ones_row, 1.0).then_inc(s_pool_consts, 1)
            pool.wait_ge(s_pool_consts, 2)

            def root(b, k):
                pool.wait_ge(s_ve[k], b + 1)
                pool.tensor_tensor(tiny[f"rstd{k}"], tiny[f"ve{k}"], powers[:, 0:1], ALU.pow).then_inc(s_rstd[k], 1)
                pool.wait_ge(s_rstd[k], b + 1)

            root(0, 1)
            root(1, 1)
            with pool.Fori(0, NB // 2 - 1) as pair:
                root(2 * pair, 2)
                root(2 * pair + 2, 1)
                root(2 * pair + 1, 2)
                root(2 * pair + 3, 1)
            root(NB - 2, 2)
            root(NB - 1, 2)

            pool.wait_ge(s_xl_ready, NB)
            for s in range(2):
                pool.memset(win[s][:, 16 * WIN:1632].bitcast(f32), 0.0).then_inc(s_win_room, 1)

            pool.wait_ge(s_win_room, 2)

            def roots(u):
                for k in range(4):
                    pool.wait_ge(s_var_eps, 4 * u + k + 1)
                    pool.tensor_tensor(tiny["rstd"], tiny["var_eps"], powers, ALU.pow).then_inc(s_root, 1)
                    pool.wait_ge(s_root, 4 * u + k + 1)

            with pool.Fori(0, 2 * NB) as u:
                roots(u)

        @block.tensor
        def _(pe):
            stats_bank, corr_bank = banks[4], banks[5]

            pe.wait_ge(s_small_in, 16 * len(small))
            pe.wait_ge(s_pool_consts, 2)
            pe.wait_ge(s_prep_qk, 1)
            pe.transpose(banks[6][:, 0:128], prep_qk, ident)
            pe.transpose(banks[6][0:9, 128:256], tiny["dw_qk_s"], ident).then_inc(s_qk_t, 1)
            pe.wait_ge(s_prep_v, 1)
            for tap in range(9):
                dst = banks[7][:, 64 * tap:64 * tap + 64] if tap < 8 else banks[0][:, 0:64]
                last = pe.transpose(dst, prep_v[0:64, 128 * tap:128 * tap + 128], ident[0:64, 0:64])
            last.then_inc(s_v_t, 1)
            pe.wait_ge(s_low_parts, 1)

            def moments(b, k):
                pe.wait_ge(s_mv[k], b + 1)
                pe.matmul(stats_bank[:, 0:1], quarter_mean, tiny[f"mv{k}"][:, 0:1], start=True, stop=True).then_inc(s_mean_mm[k], 1)
                pe.wait_ge(s_varq[k], b + 1)
                pe.matmul(stats_bank[:, 1:2], quarter_mean, tiny[f"varq{k}"], start=True, stop=True).then_inc(s_var_mm[k], 1)

            def weights(b, n, s):
                moments(b, 1)
                pe.wait_ge(s_xnsum, b + 1)
                pe.matmul(stats_bank[:, 2:3], image_mean, tiny["xnsum"], start=True, stop=True).then_inc(s_pooled_mm, 1)
                pe.wait_ge(s_pooled, b + 1)
                pe.matmul(stats_bank[:, 3:4], small["w1"], tiny["pooled"], start=True, stop=True).then_inc(s_hid_mm, 1)
                pe.wait_ge(s_hid_relu, b + 1)
                pe.matmul(stats_bank[0:1, 4:8], tiny["hid_relu"], small["w2"], start=True, stop=True).then_inc(s_logit_mm, 1)
                pe.wait_ge(s_att, b + 1)
                pe.matmul(stats_bank[:, 8:12], ones_row[0:1, :], tiny["att"][0:1, :], start=True, stop=True).then_inc(s_att_mm, 1)
                pe.wait_ge(s_mean_w, b + 1)
                pe.matmul(corr_bank[96:128, 0:96], mean_w[0:96, :], conv_w[s][0:96, :], start=True, stop=False)
                pe.matmul(corr_bank[96:128, 0:96], ident[0:96, 0:32], small["bias_row"][0:96, :], start=False, stop=True).then_inc(s_corr_mm, 1)

            def conv(b, n, s):
                pe.wait_ge(s_conv_w, b + 1)
                pe.wait_ge(s_edges, 2 * (b + 1))
                pe.wait_ge(s_support_in, 32)
                for k in range(NCH):
                    if positive(NCH * b + k - 3):
                        pe.wait_ge(s_x2_ready, NCH * b + k - 3)
                    for q in range(Q):
                        for dy in range(3):
                            row = q * (H // Q) + 4 * k + dy
                            mm = pe.matmul(banks[k % 4][32 * q:32 * q + 32, :], conv_w[s][:, 32 * dy:32 * dy + 32],
                                           x3[s][:, row * W:row * W + 512], start=dy == 0, stop=dy == 2)
                    mm.then_inc(s_conv_mm, 1)

            def slot(b, n, s, after):
                moments(b - 1, 2)
                conv(b, n, s)
                if after is not None:
                    weights(*after)

            weights(*batch(0, 0))
            conv(*batch(0, 0))
            weights(*batch(0, 1))
            with pe.Fori(0, NB // 2 - 1) as pair:
                slot(*batch(pair, 1), batch(pair + 1, 0))
                slot(*batch(pair + 1, 0), batch(pair + 1, 1))
            slot(*batch(NB // 2 - 1, 1), None)
            moments(NB - 1, 2)

            pe.wait_ge(s_spectra_in, 16)
            for m0 in range(0, 192, 8):
                if positive(m0 // 8 - 3):
                    pe.wait_ge(s_g_ready, m0 // 8 - 3)
                for m in range(m0, m0 + 8):
                    chans = dw_t[0:9, 64:128] if m < 128 else dw_t[0:9, 0:64]
                    mm = pe.matmul(banks[m0 // 8 % 4][0:WIN, 64 * (m - m0):64 * (m - m0) + 64],
                                   spec[0:9, WIN * m:WIN * m + WIN], chans, start=True, stop=True)
                mm.then_inc(s_g_mm, 1)
            pe.wait_ge(s_g_ready, 24)
            t_bank, f_bank, i_bank = banks[4], banks[6], banks[7]
            v_banks = [banks[5], banks[7]]

            def hidden_group(u, g):
                if g % 4 == 0:
                    pe.wait_ge(s_win_ready, 8 * u + g // 4 + 1)
                if g < 4:
                    if positive(16 * u):
                        pe.wait_ge(s_q_copied, 16 * u)
                    if positive(16 * u):
                        pe.wait_ge(s_prod_ready, 16 * u)
                if positive(32 * u + g - 3):
                    pe.wait_ge(s_h_ready, 32 * u + g - 3)
                w = win[g // 4 % 2]
                for i in range(4):
                    first = (4 * (g % 4) + i) * WIN
                    mm = pe.matmul(banks[g % 4][:, 128 * i:128 * i + 128], w[:, first:first + 128], hidden_w,
                                   start=True, stop=True)
                mm.then_inc(s_hidden_mm, 1)

            def v_chunk(u, half, k, jr, between):
                if k > 0:
                    pe.wait_ge(s_gated, 8 * u + 2 * k + jr - 1)
                if k == 0:
                    pe.wait_ge(s_y_ready, 8 * (u + 1))
                for s in range(2):
                    for tap in range(9):
                        dy, dx = tap // 3, tap % 3
                        row = 8 * (2 * s + jr) + dy
                        mm = pe.matmul(v_banks[jr][64 * s:64 * s + 64, :], v_w[:, 64 * tap:64 * tap + 64],
                                       at(xs[half], row * WP + 32 * k + dx, [32 * WP, 2], [WP, 8], [1, 32]),
                                       start=tap == 0, stop=tap == 8)
                        if (9 * s + tap) % 4 == 3:
                            between()
                mm.then_inc(s_v_mm, 1)

            def turn(u, k, jr):
                pe.wait_ge(s_y_norm, 4 * u + k + 1)
                if k + jr > 0:
                    pe.wait_ge(s_t_copied, 8 * u + 2 * k + jr)
                for i in range(4):
                    tr = pe.transpose(t_bank[:, 128 * i:128 * i + 128],
                                      at(Y, 8 * k + 4 * jr + i, [32, 128]), ident)
                tr.then_inc(s_turned, 1)

            def project(u, k):
                if k > 0:
                    pe.wait_ge(s_res_done, 4 * u + k)
                for jr in range(2):
                    pe.wait_ge(s_gated, 8 * u + 2 * k + jr + 1)
                    mm = pe.matmul(f_bank[64 * jr:64 * jr + 64, :], small["w_out"], gated[jr], start=True, stop=True)
                mm.then_inc(s_project_mm, 1)

            def front(u, half, tail):
                groups = iter(range(32 if u is not None else 0))

                def between():
                    g = next(groups, None)
                    if g is not None:
                        hidden_group(u, g)

                for k in range(4):
                    if tail is None:
                        for _ in range(8):
                            between()
                        continue
                    for jr in range(2):
                        v_chunk(tail, 1 - half, k, jr, between)
                    if k > 0:
                        project(tail, k - 1)
                    for jr in range(2):
                        turn(tail, k, jr)

            def spectral(u, tail):
                def inverse(n):
                    pe.wait_ge(s_prod_ready, 16 * u + n + 1)
                    if n % 2 == 0:
                        if positive(8 * u + n // 2):
                            pe.wait_ge(s_y_ready, 8 * u + n // 2)
                    if n == 0 and tail is not None:
                        pe.wait_ge(s_gated, 8 * u)
                    for lam in range(2):
                        mm = pe.matmul(i_bank[64 * lam:64 * lam + 64, 256 * (n % 2):256 * (n % 2) + 256], small["inverse"],
                                       at(prod[n % 2], 64 * lam, [128, 4], [1, 64]), start=True, stop=True)
                    mm.then_inc(s_inverse_mm, 1)

                pe.wait_ge(s_h_ready, 32 * (u + 1))
                for n in range(16):
                    for done, first, bank, free in ((s_q_mm, 0, banks[n % 2], s_q_copied), (s_k_mm, 64, banks[2 + n % 2], s_prod_ready)):
                        if positive(16 * u + n - 1):
                            pe.wait_ge(free, 16 * u + n - 1)
                        for i in range(4):
                            ch = first + 4 * n + i
                            mm = pe.matmul(bank[:, 128 * i:128 * i + 128], G[0:WIN, 128 * ch:128 * ch + 128],
                                           hwin[0:WIN, 128 * ch:128 * ch + 128], start=True, stop=True)
                        mm.then_inc(done, 1)
                    if n == 1 and tail is not None:
                        project(tail, 3)
                    if n > 0:
                        inverse(n - 1)
                inverse(15)

            front(0, 0, None)
            spectral(0, None)
            with pe.Fori(0, NB - 1) as b:
                for half in (1, 0):
                    u = 2 * b + 2 - half
                    front(u, half, u - 1)
                    spectral(u, u - 1)
            front(LAST, 1, LAST - 1)
            spectral(LAST, LAST - 1)
            front(None, 0, LAST)
            project(LAST, 3)

        @block.scalar
        def _(act):
            act.wait_ge(s_qk_t, 1)
            act.activation(hidden_w, banks[6][:, 0:128], ACT.Copy).then_inc(s_hidden_hi, 1)
            act.activation(dw_t[0:9, :], banks[6][0:9, 128:256], ACT.Copy).then_inc(s_dw_t, 1)
            act.wait_ge(s_v_t, 1)
            act.activation(v_w[:, 0:512], banks[7], ACT.Copy)
            act.activation(v_w[:, 512:576], banks[0][:, 0:64], ACT.Copy).then_inc(s_v_hi, 1)

            def weights(b, n, s):
                act.wait_ge(s_shift1, b + 1)
                act.wait_ge(s_xq_in[s], 64 * (n + 1))
                act.activation(xnf, xq[s], ACT.Identity, bias=tiny["shift1"], scale=tiny["rstd1"],
                               accum_out=tiny["xnsum"]).then_inc(s_xnsum, 1)
                act.wait_ge(s_pooled, b + 1)
                act.activation(tiny["gate_exp"], tiny["pooled"], ACT.Exp, scale=-1.0).then_inc(s_gate_exp, 1)
                act.wait_ge(s_neg_max_t, b + 1)
                act.activation(tiny["exps"][0:1, :], stats_psum[0:1, 4:8], ACT.Exp, scale=1.0 / TEMPERATURE,
                               bias=tiny["neg_max_t"][0:1, :], accum_out=tiny["exp_sum"][0:1, :]).then_inc(s_exps, 1)

            def normalise(b, n, s):
                act.wait_ge(s_shift2, b + 1)
                act.wait_ge(s_xn_out, 128 * b + 32)
                rows = lambda a: a.rearrange("p (h w) -> p h w", w=W)
                padded = xh.rearrange("p (h w) -> p h w", w=WP)[:, :, 1:W + 1]
                act.activation(padded, rows(xq[s]), ACT.Identity, bias=tiny["shift2"], scale=tiny["scale2"]).then_inc(s_xh_ready, 1)
                act.wait_ge(s_xnsum, b + 2 if not (isinstance(b, int) and b >= NB - 1) else NB)
                act.activation(xnf, xq[s], ACT.Identity, bias=tiny["shift2"], scale=tiny["scale2"]).then_inc(s_xnf_ready, 1)

            stats_psum = banks[4]
            weights(*batch(0, 0))
            act.wait_ge(s_xn_out, 32)
            weights(*batch(0, 1))
            with act.Fori(0, NB // 2 - 1) as pair:
                for s in range(2):
                    normalise(*batch(pair, s))
                    weights(*batch(pair + 1, s))
            normalise(*batch(NB // 2 - 1, 0))
            normalise(*batch(NB // 2 - 1, 1))

            g_rows = G.rearrange("p (c m) -> p c m", m=128)
            for i in range(24):
                act.wait_ge(s_g_mm, i + 1)
                src = banks[i % 4][0:WIN, :].rearrange("p (m c) -> p c m", m=8)
                if i < 16:
                    act.activation(g_rows[0:WIN, 64:128, 8 * i:8 * i + 8], src, ACT.Copy).then_inc(s_g_ready, 1)
                else:
                    act.activation(g_rows[0:WIN, 0:64, 8 * i - 128:8 * i - 120], src, ACT.Copy)
                    act.activation(g_rows[0:WIN, 0:64, 8 * i - 64:8 * i - 56], src, ACT.Copy).then_inc(s_g_ready, 1)

            h_rows = hwin.rearrange("p (c j) -> p c j", j=128)
            Y_out = Y.rearrange("p (s c j) -> p c s j", s=2, j=32)
            Y_sq = Y.rearrange("p (s c j) -> p s c j", s=2, j=32)

            def windows_out(u, g):
                pr, k = g // 4, g % 4
                first = 64 * (pr // 4) + 32 * (pr // 2 % 2) + 8 * k + 4 * (pr % 2)
                act.wait_ge(s_hidden_mm, 32 * u + g + 1)
                act.activation(h_rows[0:WIN, :, first:first + 4],
                               banks[g % 4][0:WIN, :].rearrange("p (i c) -> p c i", i=4), ACT.Copy).then_inc(s_h_ready, 1)

            def square(u, k):
                act.wait_ge(s_y_centred, 4 * u + k + 1)
                if k > 0:
                    act.wait_ge(s_sq_sums, 4 * u + k)
                act.activation(squares.rearrange("p (s c j) -> p s c j", s=2, j=8), Y_sq[:, :, :, 8 * k:8 * k + 8],
                               ACT.Square).then_inc(s_squared, 1)

            def turned_out(u, k, jr):
                act.wait_ge(s_turned, 8 * u + 2 * k + jr + 1)
                if k > 0:
                    act.wait_ge(s_project_mm, 4 * u + k)
                for lam in range(2):
                    ins = act.activation(at(gated[jr], 256 * lam, [32, 8], [8, 4], [1, 8]),
                                         at(banks[4], 64 * lam, [8, 8], [128, 4], [1, 8]), ACT.Identity,
                                         bias=tiny["v_shift"], scale=tiny["v_scale"])
                ins.then_inc(s_t_copied, 1)

            def front(u, tail):
                groups = iter(range(32 if u is not None else 0))

                def some(n):
                    for _ in range(n):
                        g = next(groups, None)
                        if g is not None:
                            windows_out(u, g)

                for k in range(4):
                    if tail is None:
                        some(8)
                        continue
                    some(3)
                    if k == 0:
                        square(tail, 0)
                    some(3)
                    if k < 3:
                        square(tail, k + 1)
                    some(2)
                    for jr in range(2):
                        turned_out(tail, k, jr)

            def spectral(u):
                for n in range(16):
                    act.wait_ge(s_q_mm, 16 * u + n + 1)
                    if positive(16 * u + n - 1):
                        act.wait_ge(s_prod_ready, 16 * u + n - 1)
                    act.activation(q_sb[n % 2], banks[n % 2], ACT.Copy).then_inc(s_q_copied, 1)
                    if n % 2 == 1 and n >= 3:
                        inverse_out(u, n // 2 - 1)
                inverse_out(u, 7)

            def inverse_out(u, e):
                act.wait_ge(s_inverse_mm, 16 * u + 2 * e + 2)
                act.activation(Y_out[:, 8 * e:8 * e + 8, :, :], banks[7].rearrange("p (c s j) -> p c s j", s=2, j=32),
                               ACT.Copy).then_inc(s_y_ready, 1)

            front(0, None)
            spectral(0)
            with act.Fori(0, NB - 1) as b:
                for half in (1, 0):
                    u = 2 * b + 2 - half
                    front(u, u - 1)
                    spectral(u)
            front(LAST, LAST - 1)
            spectral(LAST)
            front(None, LAST)

        @block.vector
        def _(dve):
            T = tiny
            dve.wait_ge(s_small_in, 16 * len(small))
            dve.wait_ge(s_pads_zero, 2)
            dve.tensor_scalar(T["gammas"], small["gamma"], float(1 / np.sqrt(np.float32(1 + EPS))), None, ALU.mult).then_inc(s_prep, 1)
            dve.wait_ge(s_prep, 1)
            dve.tensor_reduce(T["qk_max"], small["hidden_qk"], X_AXIS, ALU.max, apply_absolute_value=True).then_inc(s_prep, 1)
            dve.wait_ge(s_prep, 2)
            dve.tensor_scalar(T["qk_max"], T["qk_max"], TINY, None, ALU.max).then_inc(s_prep, 1)
            dve.wait_ge(s_prep, 3)
            dve.reciprocal(T["qk_inv"], T["qk_max"]).then_inc(s_prep, 1)
            dve.wait_ge(s_prep, 4)
            dve.tensor_scalar(T["qk_back"], T["qk_max"], 1 / X_SCALE, None, ALU.mult).then_inc(s_prep, 1)
            dve.wait_ge(s_prep, 5)
            for g in range(4):
                dve.tensor_scalar(prep_qk[:, 32 * g:32 * g + 32], small["hidden_qk"], T["qk_inv"], None, ALU.mult).then_inc(s_prep, 1)
                dve.wait_ge(s_prep, 6 + g)
            dve.tensor_scalar(T["dw_qk_s"], small["dw_qk"], T["qk_back"], None, ALU.mult).then_inc(s_prep_qk, 1)
            dve.wait_ge(s_prep_qk, 1)
            dve.tensor_reduce(T["v_max"], small["hidden_v"], X_AXIS, ALU.max, apply_absolute_value=True).then_inc(s_prep, 1)
            dve.wait_ge(s_prep, 10)
            dve.tensor_scalar(T["v_max"], T["v_max"], TINY, None, ALU.max).then_inc(s_prep, 1)
            dve.wait_ge(s_prep, 11)
            dve.reciprocal(T["v_inv"], T["v_max"]).then_inc(s_prep, 1)
            dve.wait_ge(s_prep, 12)
            dve.tensor_reduce(T["d_max"], small["dw_v"], X_AXIS, ALU.max, apply_absolute_value=True).then_inc(s_prep, 1)
            dve.wait_ge(s_prep, 13)
            dve.tensor_scalar(T["d_max"], T["d_max"], TINY, None, ALU.max).then_inc(s_prep, 1)
            dve.wait_ge(s_prep, 14)
            dve.reciprocal(T["d_inv"], T["d_max"]).then_inc(s_prep, 1)
            dve.wait_ge(s_prep, 15)
            dve.tensor_scalar(T["dw_v_n"], small["dw_v"], T["d_inv"], None, ALU.mult).then_inc(s_prep, 1)
            dve.wait_ge(s_prep, 16)
            for tap in range(9):
                for g in range(4):
                    ins = dve.tensor_scalar(prep_v[:, 128 * tap + 32 * g:128 * tap + 32 * g + 32], small["hidden_v"],
                                            T["v_inv"], T["dw_v_n"][:, tap:tap + 1], ALU.mult, ALU.mult)
            ins.then_inc(s_prep_v, 1)
            dve.tensor_scalar(T["v_back"], T["v_max"], T["d_max"], 1 / X_SCALE, ALU.mult, ALU.mult).then_inc(s_prep, 1)
            dve.wait_ge(s_prep, 17)
            dve.tensor_scalar(T["v_scale"], small["norm_w"], T["v_back"], None, ALU.mult)
            dve.tensor_scalar(T["v_shift"], small["norm_b"], T["v_back"], None, ALU.mult).then_inc(s_v_consts, 1)
            dve.wait_ge(s_hidden_hi, 1)
            dve.tensor_tensor(hidden_w[64:128, :], banks[6][64:128, 0:128], hidden_w[64:128, :], ALU.subtract)
            dve.wait_ge(s_v_hi, 1)
            dve.tensor_tensor(v_w[64:128, 0:512], banks[7][64:128, :], v_w[64:128, 0:512], ALU.subtract)
            dve.tensor_tensor(v_w[64:128, 512:576], banks[0][64:128, 0:64], v_w[64:128, 512:576], ALU.subtract).then_inc(s_low_parts, 1)

            stats_bank, corr_bank = banks[4], banks[5]

            def moments(b, k, stats):
                dve.wait_ge(s_st[k], NCH * (b + 1))
                dve.memset(T[f"dev{k}"], 0.0)
                dve.bn_aggr(T[f"mv{k}"], stats).then_inc(s_mv[k], 1)
                dve.wait_ge(s_mv[k], b + 1)
                dve.wait_ge(s_mean_mm[k], b + 1)
                dve.tensor_copy(T[f"mean{k}"], stats_bank[:, 0:1])
                dve.tensor_tensor(T[f"dev{k}"], T[f"mv{k}"][:, 0:1], stats_bank[:, 0:1], ALU.subtract).then_inc(s_dev[k], 1)
                dve.wait_ge(s_dev[k], b + 1)
                dve.scalar_tensor_tensor(T[f"varq{k}"], T[f"dev{k}"], T[f"dev{k}"], T[f"mv{k}"][:, 1:2], ALU.mult, ALU.add).then_inc(s_varq[k], 1)
                dve.wait_ge(s_varq[k], b + 1)
                dve.wait_ge(s_var_mm[k], b + 1)
                dve.tensor_scalar(T[f"ve{k}"], stats_bank[:, 1:2], EPS, None, ALU.add).then_inc(s_ve[k], 1)
                dve.wait_ge(s_ve[k], b + 1)
                dve.wait_ge(s_rstd[k], b + 1)

            def edges(b, n, s):
                dve.wait_ge(s_x3_in[s], 48 * (n + 1))
                dve.memset(at(x3[s][0:32, :], W, [W, H]), 0.0).then_inc(s_edges, 1)
                dve.memset(at(x3[s][64:96, :], 2 * W - 1, [W, H]), 0.0).then_inc(s_edges, 1)

            def weights(b, n, s):
                dve.wait_ge(s_xq_in[s], 64 * (n + 1))
                for k in range(NCH):
                    dve.bn_stats(st1[:, 6 * k:6 * k + 6], xq[s][:, 512 * k:512 * k + 512]).then_inc(s_st[1], 1)
                moments(b, 1, st1)
                dve.scalar_tensor_tensor(T["shift1"], T["mean1"], -1.0, T["rstd1"], ALU.mult, ALU.mult).then_inc(s_shift1, 1)
                dve.wait_ge(s_shift1, b + 1)
                dve.wait_ge(s_pooled_mm, b + 1)
                dve.tensor_copy(T["pooled"], stats_bank[:, 2:3]).then_inc(s_pooled, 1)
                dve.wait_ge(s_hid_mm, b + 1)
                dve.tensor_scalar(T["hid"], stats_bank[:, 3:4], T["gammas"], small["beta"], ALU.mult, ALU.add).then_inc(s_hid, 1)
                dve.wait_ge(s_hid, b + 1)
                dve.tensor_scalar(T["hid_relu"], T["hid"], 0.0, None, ALU.max).then_inc(s_hid_relu, 1)
                dve.wait_ge(s_logit_mm, b + 1)
                dve.tensor_reduce(T["neg_max"][0:1, :], stats_bank[0:1, 4:8], X_AXIS, ALU.max, negate=True).then_inc(s_neg_max, 1)
                dve.wait_ge(s_neg_max, b + 1)
                dve.tensor_scalar(T["neg_max_t"][0:1, :], T["neg_max"][0:1, :], 1.0 / TEMPERATURE, None, ALU.mult).then_inc(s_neg_max_t, 1)
                dve.wait_ge(s_gate_exp, b + 1)
                dve.tensor_scalar(T["gate_den"], T["gate_exp"], 1.0, None, ALU.add).then_inc(s_gate_den, 1)
                dve.wait_ge(s_gate_den, b + 1)
                dve.reciprocal(T["gate"], T["gate_den"]).then_inc(s_gate, 1)
                dve.wait_ge(s_gate, b + 1)
                dve.tensor_scalar(T["chan_scale"], T["gate"], T["rstd1"], None, ALU.mult).then_inc(s_chan_scale, 1)
                dve.wait_ge(s_exps, b + 1)
                dve.reciprocal(T["exp_inv"][0:1, :], T["exp_sum"][0:1, :]).then_inc(s_exp_inv, 1)
                dve.wait_ge(s_exp_inv, b + 1)
                dve.tensor_scalar(T["att"][0:1, :], T["exps"][0:1, :], T["exp_inv"][0:1, :], None, ALU.mult).then_inc(s_att, 1)
                dve.wait_ge(s_att_mm, b + 1)
                dve.tensor_copy(T["att_all"], stats_bank[:, 8:12]).then_inc(s_att_all, 1)
                dve.wait_ge(s_att_all, b + 1)
                agg, dyn = T["agg"][0:96, :], small["dyn_w"][0:96, :]
                dve.tensor_scalar(agg, dyn[:, 0:3], T["att_all"][0:96, 0:1], None, ALU.mult).then_inc(s_agg, 1)
                dve.wait_ge(s_agg, 4 * b + 1)
                for k in range(1, 4):
                    dve.scalar_tensor_tensor(agg, dyn[:, 3 * k:3 * k + 3], T["att_all"][0:96, k:k + 1], agg, ALU.mult, ALU.add).then_inc(s_agg, 1)
                    dve.wait_ge(s_agg, 4 * b + 1 + k)
                dve.wait_ge(s_chan_scale, b + 1)
                for dy in range(3):
                    dve.tensor_scalar(conv_w[s][0:96, 32 * dy:32 * dy + 32], small["conv1"][0:96, :], agg[:, dy:dy + 1],
                                      T["chan_scale"][0:96, :], ALU.mult, ALU.mult)
                dve.tensor_scalar(mean_w, small["tap_group"], T["mean1"], -1.0, ALU.mult, ALU.mult).then_inc(s_mean_w, 1)
                dve.wait_ge(s_corr_mm, b + 1)
                dve.tensor_copy(conv_w[s][96:128, :], corr_bank[96:128, 0:96]).then_inc(s_conv_w, 1)
                edges(b, n, s)

            def conv(b, n, s):
                for k in range(NCH):
                    dve.wait_ge(s_conv_mm, NCH * b + k + 1)
                    piece = xq[s][:, 512 * k:512 * k + 512]
                    dve.tensor_tensor(piece, banks[k % 4], piece, ALU.add).then_inc(s_x2_ready, 1)
                    if k > 0:
                        second_stats(b, s, k - 1)
                second_stats(b, s, NCH - 1)

            def second_stats(b, s, k):
                dve.wait_ge(s_x2_ready, NCH * b + k + 1)
                dve.bn_stats(st2[:, 6 * k:6 * k + 6], xq[s][:, 512 * k:512 * k + 512]).then_inc(s_st[2], 1)

            def normalise(b, n, s):
                moments(b, 2, st2)
                dve.tensor_scalar(T["scale2"], T["rstd2"], X_SCALE, None, ALU.mult).then_inc(s_scale2, 1)
                dve.wait_ge(s_scale2, b + 1)
                dve.scalar_tensor_tensor(T["shift2"], T["mean2"], -1.0, T["scale2"], ALU.mult, ALU.mult).then_inc(s_shift2, 1)

            def low(b):
                dve.wait_ge(s_xnf_ready, b + 1)
                padded = lambda a: a.rearrange("p (h w) -> p h w", w=WP)[:, :, 1:W + 1]
                dve.tensor_tensor(padded(xl), xnf.rearrange("p (h w) -> p h w", w=W), padded(xh), ALU.subtract).then_inc(s_xl_ready, 1)

            weights(*batch(0, 0))
            conv(*batch(0, 0))
            weights(*batch(0, 1))
            with dve.Fori(0, NB // 2 - 1) as pair:
                for prev, here, after in ((batch(pair, 0), batch(pair, 1), batch(pair + 1, 0)),
                                          (batch(pair, 1), batch(pair + 1, 0), batch(pair + 1, 1))):
                    normalise(*prev)
                    low(prev[0])
                    conv(*here)
                    weights(*after)
            normalise(*batch(NB // 2 - 1, 0))
            low(NB - 2)
            conv(*batch(NB // 2 - 1, 1))
            normalise(*batch(NB // 2 - 1, 1))
            low(NB - 1)

            Y4 = Y.rearrange("p (s c j) -> p s c j", s=2, j=32)
            sq4 = squares.rearrange("p (s c j) -> p s c j", s=2, j=8)
            by_chan = lambda a: a.rearrange("p s c j -> p s j c")
            over = lambda a: a.rearrange("p (s j) -> p s j", s=2).unsqueeze(2).broadcast_to([128, 2, 64, 8])

            def window(u, half, r, b=None):
                if positive(32 * u + 4 * (r - 1)):
                    dve.wait_ge(s_hidden_mm, 32 * u + 4 * (r - 1))
                if r == 0:
                    dve.wait_ge(s_xs_in[half], 64 * (b + 1))
                dve.tensor_copy(win[r % 2][:, 0:16 * WIN].rearrange("p (j y x) -> p j y x", y=10, x=10),
                                     at(xs[half], 8 * r * WP, [8, 16], [WP, 10], [1, 10])).then_inc(s_win_ready, 1)

            def centre(u, k):
                if k == 0:
                    dve.wait_ge(s_y_ready, 8 * (u + 1))
                piece = Y4[:, :, :, 8 * k:8 * k + 8]
                dve.tensor_reduce(T["sums"].rearrange("p (s j) -> p s j", s=2), by_chan(piece), X_AXIS, ALU.add).then_inc(s_sums, 1)
                dve.wait_ge(s_sums, 4 * u + k + 1)
                dve.tensor_scalar(T["neg_mu"], T["sums"], -1.0 / 64, None, ALU.mult).then_inc(s_neg_mu, 1)
                dve.wait_ge(s_neg_mu, 4 * u + k + 1)
                dve.tensor_tensor(piece, piece, over(T["neg_mu"]), ALU.add).then_inc(s_y_centred, 1)

            def variance(u, k):
                dve.wait_ge(s_squared, 4 * u + k + 1)
                dve.tensor_reduce(T["sq_sums"].rearrange("p (s j) -> p s j", s=2), by_chan(sq4), X_AXIS, ALU.add).then_inc(s_sq_sums, 1)
                dve.wait_ge(s_sq_sums, 4 * u + k + 1)
                if k > 0:
                    dve.wait_ge(s_root, 4 * u + k)
                dve.tensor_scalar(T["var_eps"], T["sq_sums"], 1.0 / 64, EPS, ALU.mult, ALU.add).then_inc(s_var_eps, 1)

            def scale(u, k):
                piece = Y4[:, :, :, 8 * k:8 * k + 8]
                dve.wait_ge(s_root, 4 * u + k + 1)
                dve.wait_ge(s_y_centred, 4 * u + k + 1)
                dve.tensor_tensor(piece, piece, over(T["rstd"]), ALU.mult).then_inc(s_y_norm, 1)

            def gate(u, k, jr):
                dve.wait_ge(s_t_copied, 8 * u + 2 * k + jr + 1)
                dve.wait_ge(s_v_mm, 8 * u + 2 * k + jr + 1)
                dve.tensor_tensor(gated[jr], gated[jr], [banks[5], banks[7]][jr], ALU.mult).then_inc(s_gated, 1)

            def residual(u, k):
                dve.wait_ge(s_project_mm, 4 * u + k + 1)
                if k == 0:
                    dve.wait_ge(s_res_in, 64 * (u + 1))
                piece = at(res, 32 * k, [1024, 2], [W, 8], [1, 32])
                dve.tensor_tensor(piece, banks[6].rearrange("p (l r w) -> p l r w", l=2, r=8), piece, ALU.add).then_inc(s_res_done, 1)

            def front(u, half, tail):
                rows = iter(range(2, 8)) if u is not None else iter(())

                def windows(n):
                    for _ in range(n):
                        r = next(rows, None)
                        if r is not None:
                            window(u, half, r)

                if tail is None:
                    windows(6)
                    return
                centre(tail, 0)
                centre(tail, 1)
                variance(tail, 0)
                windows(1)
                scale(tail, 0)
                windows(1)
                for k in range(4):
                    if k + 2 < 4:
                        centre(tail, k + 2)
                    if k + 1 < 4:
                        variance(tail, k + 1)
                    windows(min(k, 1))
                    if k + 1 < 4:
                        scale(tail, k + 1)
                    windows(min(k, 1))
                    for jr in range(2):
                        gate(tail, k, jr)
                    if k > 0:
                        residual(tail, k - 1)

            def spectral(u, tail, nxt):
                for n in range(16):
                    dve.wait_ge(s_q_copied, 16 * u + n + 1)
                    dve.wait_ge(s_k_mm, 16 * u + n + 1)
                    if positive(16 * u + n - 1):
                        dve.wait_ge(s_inverse_mm, 16 * u + n - 1)
                    dve.tensor_tensor(prod[n % 2], banks[2 + n % 2], q_sb[n % 2], ALU.mult).then_inc(s_prod_ready, 1)
                    if n == 1 and tail is not None:
                        residual(tail, 3)
                    if nxt is not None and n in (8, 10):
                        window(nxt[0], nxt[1], (n - 8) // 2, nxt[2])

            dve.wait_ge(s_g_ready, 24)
            dve.wait_ge(s_win_room, 2)
            window(0, 0, 0, 0)
            window(0, 0, 1, 0)
            front(0, 0, None)
            spectral(0, None, (1, 1, 0))
            with dve.Fori(0, NB - 1) as b:
                for half in (1, 0):
                    u = 2 * b + 2 - half
                    front(u, half, u - 1)
                    spectral(u, u - 1, (u + 1, 1 - half, b + 1))
            front(LAST, 1, LAST - 1)
            spectral(LAST, LAST - 1, None)
            front(None, 0, LAST)
            residual(LAST, 3)


def kernel(**inputs):
    import concourse.bacc as bacc
    from concourse.bass_utils import run_bass_kernel_spmd

    a = {n: np.asarray(v) for n, v in inputs.items()}

    def padded(v, rows):
        return np.pad(v, ((0, rows - v.shape[0]), (0, 0)))

    def column(v):
        return v.reshape(-1, 1)

    hidden, dw = a["L1_conv_w_hidden"], a["L1_conv_w_dw"].reshape(192, 9)
    w_out = a["L1_conv_w_out"].T
    zero = np.zeros_like(w_out)
    dyn = a["L0_conv_weight"].reshape(4, 32, 3, 3)
    bias_row = np.zeros((96, 96), np.float32)
    bias_row[3, 32:64] = a["L0_conv_conv1_b"]
    arrays = {
        "x": a["x"],
        "w1": np.pad(a["L0_conv_att_w1"].T, ((0, 96), (0, 111))),
        "w2": padded(a["L0_conv_att_w2"].T, 128),
        "dyn_w": dyn.transpose(3, 1, 0, 2).reshape(96, 12),
        "conv1": np.tile(a["L0_conv_conv1_w"].T, (3, 1)),
        "bias_row": bias_row,
        "gamma": padded(column(a["L0_conv_bn_gamma"]), 128),
        "beta": padded(column(a["L0_conv_bn_beta"]), 128),
        "hidden_qk": hidden[0:128], "dw_qk": dw[0:128],
        "hidden_v": np.tile(hidden[128:], (2, 1)), "dw_v": np.tile(dw[128:], (2, 1)),
        "norm_w": np.tile(column(a["L1_conv_norm_w"]), (2, 1)), "norm_b": np.tile(column(a["L1_conv_norm_b"]), (2, 1)),
        "w_out": np.block([[w_out, zero], [zero, w_out]]),
        **constants(),
    }
    arrays = {n: np.ascontiguousarray(v) for n, v in arrays.items()}
    nc = bacc.Bacc("TRN2", target_bir_lowering=False, num_devices=1)
    t = {n: nc.dram_tensor(f"{n}_in", v.shape, mybir.dt.from_np(v.dtype), kind="ExternalInput").ap() for n, v in arrays.items()}
    out = nc.dram_tensor("out", a["x"].shape, mybir.dt.float32, kind="ExternalOutput").ap()
    build(nc, t, out)
    r = run_bass_kernel_spmd(nc, [{f"{n}_in": v for n, v in arrays.items()}], core_ids=[0])
    return r.results[0]["out"]
```

```python
from contextlib import ExitStack
from itertools import islice

import numpy as np

import concourse.bass as bass
from concourse import mybir

EPS = 1e-5
TEMPERATURE = 30.0
X_SCALE = 256.0
TINY = 1e-30


def constants():
    p = np.arange(128)
    same_channel = (p[:, None] % 32 == p[None, :] % 32).astype(np.float32)
    out = {"identity": np.eye(128, dtype=np.float32), "quarter_mean": same_channel / 4,
           "image_mean": same_channel / (4 * 4096)}
    group = np.zeros((128, 32), np.float32)
    for g in range(3):
        group[32 * g:32 * g + 32, g] = 1
    out["tap_group"] = group
    support = np.zeros((32, 130, 128), np.float32)
    support[0, 1:129, 1:] = 1
    support[1, 1:129, :] = 1
    support[2, 1:129, :127] = 1
    support[3] = 1
    out["support"] = support.reshape(32, 130 * 128)
    u, v = np.meshgrid(np.arange(8), np.arange(8), indexing="ij")
    u, v = u.ravel(), v.ravel()
    spectra = np.zeros((9, 3, 64, 10, 10), np.float64)
    for dy in range(3):
        for dx in range(3):
            for y in range(8):
                for x in range(8):
                    a = 2 * np.pi * ((u * y + v * x) % 8) / 8
                    spectra[3 * dy + dx, :, :, y + dy, x + dx] = [np.cos(a), np.sin(a), np.cos(a) + np.sin(a)]
    out["spectra"] = spectra.reshape(9, 192 * 100).astype(np.float32)
    a = 2 * np.pi * ((u[:, None] * u[None, :] + v[:, None] * v[None, :]) % 8) / 8
    out["inverse"] = (np.concatenate([np.cos(a) + np.sin(a), np.sin(a) - np.cos(a)]) / 64).astype(np.float32)
    return out


def build(nc, t, out):
    f32, f16 = mybir.dt.float32, mybir.dt.float16
    ALU, ACT, X_AXIS = mybir.AluOpType, mybir.ActivationFunctionType, mybir.AxisListType.X
    x = t["x"]
    NB, C, H, W = x.shape
    PIX = H * W
    Q = 4
    QPIX = PIX // Q
    NCH = QPIX // 512
    WP = W + 2
    HALF = H // 2 + 2
    WIN = 100
    LAST = 2 * NB - 1

    def dram(name, shape, dt):
        return nc.dram_tensor(name, shape, dt, kind="Internal").ap()

    x2_d = dram("x2_d", [NB, C, PIX], f32)
    xn_d = dram("xn_d", [NB, 2, C, H + 2, WP], f16)

    ctx = ExitStack()
    with ctx:
        def sb(name, cols, dt=f32, rows=128):
            return ctx.enter_context(nc.sbuf_tensor(name, [rows, cols], dt))[:, :]

        banks = [ctx.enter_context(nc.psum_tensor(f"bank{i}", [128, 512], f32))[:, :] for i in range(8)]
        def semaphore(name):
            return ctx.enter_context(nc.semaphore(name))

        def positive(value):
            return not isinstance(value, int) or value > 0

        s_small_in = semaphore("small_in")
        s_support_in = semaphore("support_in")
        s_x3_in = [semaphore(f"x3_in{s}") for s in range(2)]
        s_xq_in = [semaphore(f"xq_in{s}") for s in range(2)]
        s_x2_out = [semaphore(f"x2_out{s}") for s in range(2)]
        s_xn_out = semaphore("xn_out")
        s_spectra_in = semaphore("spectra_in")
        s_xs_in = [semaphore(f"xs_in{s}") for s in range(2)]
        s_res_in = semaphore("res_in")
        s_out_stored = semaphore("out_stored")
        s_x3_zero = semaphore("x3_zero")
        s_pads_zero = semaphore("pads_zero")
        s_pool_consts = semaphore("pool_consts")
        s_win_room = semaphore("win_room")
        s_prep = semaphore("prep")
        s_prep_qk = semaphore("prep_qk")
        s_prep_v = semaphore("prep_v")
        s_v_consts = semaphore("v_consts")
        s_qk_t = semaphore("qk_t")
        s_v_t = semaphore("v_t")
        s_hidden_hi = semaphore("hidden_hi")
        s_dw_t = semaphore("dw_t")
        s_v_hi = semaphore("v_hi")
        s_low_parts = semaphore("low_parts")
        s_g_mm = semaphore("g_mm")
        s_g_ready = semaphore("g_ready")
        s_st = {k: semaphore(f"st{k}") for k in (1, 2)}
        s_mv = {k: semaphore(f"mv{k}") for k in (1, 2)}
        s_mean_mm = {k: semaphore(f"mean_mm{k}") for k in (1, 2)}
        s_dev = {k: semaphore(f"dev{k}") for k in (1, 2)}
        s_varq = {k: semaphore(f"varq{k}") for k in (1, 2)}
        s_var_mm = {k: semaphore(f"var_mm{k}") for k in (1, 2)}
        s_ve = {k: semaphore(f"ve{k}") for k in (1, 2)}
        s_rstd = {k: semaphore(f"rstd{k}") for k in (1, 2)}
        s_shift1 = semaphore("shift1")
        s_xnsum = semaphore("xnsum")
        s_pooled_mm = semaphore("pooled_mm")
        s_pooled = semaphore("pooled")
        s_hid_mm = semaphore("hid_mm")
        s_hid = semaphore("hid")
        s_hid_relu = semaphore("hid_relu")
        s_logit_mm = semaphore("logit_mm")
        s_neg_max = semaphore("neg_max")
        s_neg_max_t = semaphore("neg_max_t")
        s_gate_exp = semaphore("gate_exp")
        s_gate_den = semaphore("gate_den")
        s_gate = semaphore("gate")
        s_chan_scale = semaphore("chan_scale")
        s_exps = semaphore("exps")
        s_exp_inv = semaphore("exp_inv")
        s_att = semaphore("att")
        s_att_mm = semaphore("att_mm")
        s_att_all = semaphore("att_all")
        s_agg = semaphore("agg")
        s_mean_w = semaphore("mean_w")
        s_corr_mm = semaphore("corr_mm")
        s_conv_w = semaphore("conv_w")
        s_edges = semaphore("edges")
        s_conv_mm = semaphore("conv_mm")
        s_x2_ready = semaphore("x2_ready")
        s_scale2 = semaphore("scale2")
        s_shift2 = semaphore("shift2")
        s_xh_ready = semaphore("xh_ready")
        s_xnf_ready = semaphore("xnf_ready")
        s_xl_ready = semaphore("xl_ready")
        s_win_ready = semaphore("win_ready")
        s_hidden_mm = semaphore("hidden_mm")
        s_h_ready = semaphore("h_ready")
        s_q_mm = semaphore("q_mm")
        s_q_copied = semaphore("q_copied")
        s_k_mm = semaphore("k_mm")
        s_prod_ready = semaphore("prod_ready")
        s_inverse_mm = semaphore("inverse_mm")
        s_y_ready = semaphore("y_ready")
        s_part_sums = semaphore("part_sums")
        s_sums = semaphore("sums")
        s_neg_mu = semaphore("neg_mu")
        s_y_centred = semaphore("y_centred")
        s_squared = semaphore("squared")
        s_sq_sums = semaphore("sq_sums")
        s_var_eps = semaphore("var_eps")
        s_root = semaphore("root")
        s_y_norm = semaphore("y_norm")
        s_turned = semaphore("turned")
        s_t_copied = semaphore("t_copied")
        s_v_mm = semaphore("v_mm")
        s_gated = semaphore("gated")
        s_project_mm = semaphore("project_mm")
        s_res_done = semaphore("res_done")

        def at(ap, offset, *dims):
            return bass.AP(tensor=ap.tensor, offset=ap.offset + offset, ap=[ap.ap[0]] + [list(d) for d in dims])

        v_banks = [banks[5], banks[7], banks[3]]

        WORDS = 53200
        arena = sb("arena", WORDS)
        top = [0]

        def take(cols, dt=f32):
            words = cols if dt == f32 else (cols + 1) // 2
            a = arena[:, top[0]:top[0] + words]
            top[0] += words
            assert top[0] <= WORDS, top[0]
            return a if dt == f32 else a.bitcast(dt)

        small = {n: take(t[n].shape[1]) for n in ("identity", "inverse", "w_out")}
        ident = small["identity"]
        hidden_w = take(128, f16)
        v_w = take(9 * 64, f16)
        powers = take(16)
        tiny = {n: take(c) for n, c in (("v_scale", 1), ("v_shift", 1), ("part_sums", 64), ("neg_mu", 64),
                                        ("sq_sums", 32), ("var_eps", 32), ("rstd", 32))}
        phases = top[0]

        x3 = [take((H + 2) * W) for _ in range(2)]
        xq = [take(QPIX) for _ in range(2)]
        xnf = take(QPIX)
        xh, xl = take(QPIX // W * WP, f16), take(QPIX // W * WP, f16)
        prep_qk, prep_v = xnf[:, 0:128], xnf[:, 128:128 + 9 * 128]
        small |= {n: take(t[n].shape[1]) for n in
                  ("quarter_mean", "image_mean", "tap_group", "w1", "w2", "dyn_w", "conv1", "bias_row", "gamma", "beta",
                   "hidden_qk", "dw_qk", "hidden_v", "dw_v", "norm_w", "norm_b")}
        quarter_mean, image_mean = small["quarter_mean"], small["image_mean"]
        ones_row = take(128)
        conv_w = [take(96) for s in range(2)]
        mean_w = take(32)
        st1, st2 = take(6 * NCH), take(6 * NCH)
        tiny |= {n: take(c) for n, c in (
            ("mv1", 2), ("mean1", 1), ("dev1", 1), ("varq1", 1), ("ve1", 1), ("rstd1", 1), ("shift1", 1),
            ("mv2", 2), ("mean2", 1), ("dev2", 1), ("varq2", 1), ("ve2", 1), ("rstd2", 1), ("scale2", 1), ("shift2", 1),
            ("xnsum", 1), ("pooled", 1), ("hid", 1), ("hid_relu", 1), ("neg_max", 1), ("neg_max_t", 1), ("exps", 4),
            ("exp_sum", 1), ("exp_inv", 1), ("att", 4), ("att_all", 4), ("gate_exp", 1), ("gate_den", 1), ("gate", 1),
            ("chan_scale", 1), ("agg", 3), ("gammas", 1), ("qk_max", 1), ("qk_inv", 1), ("qk_back", 1),
            ("v_max", 1), ("v_inv", 1), ("d_max", 1), ("d_inv", 1), ("v_back", 1), ("dw_qk_s", 9), ("dw_v_n", 9))}
        phase_a_end = top[0]

        top[0] = phases
        hwin = take(128 * 128)
        Y = take(64 * 64)
        spec = arena[:, phases:phases + 192 * WIN]
        G = take(128 * 128)
        xs = [take(HALF * WP, f16) for _ in range(2)]
        q_sb = [take(512) for _ in range(2)]
        squares = arena[:, top[0] - 1024:top[0]]
        prod = [take(512) for _ in range(2)]
        gated = [take(512) for _ in range(2)]
        res = take(2048)
        win_at = top[0]
        win = [take(1632, f16) for _ in range(2)]
        dw_t = arena[:, max(win_at, phase_a_end):max(win_at, phase_a_end) + 128]
        assert max(win_at, phase_a_end) + 128 <= win_at + 800
        block = ctx.enter_context(nc.Block())

        def batch(pair, odd):
            return 2 * pair + odd, pair, odd

        @block.sync
        def _(sp):
            for name in small:
                rows = t[name].shape[0]
                sp.dma_start(small[name][0:rows, :], t[name]).then_inc(s_small_in, 16)

            def load_x3(b, n, s):
                flat = x[b].rearrange("c h w -> c (h w)")
                sp.dma_start(x3[s][0:32, W + 1:W + PIX], flat[:, 0:PIX - 1]).then_inc(s_x3_in[s], 16)
                sp.dma_start(x3[s][32:64, W:W + PIX], flat).then_inc(s_x3_in[s], 16)
                sp.dma_start(x3[s][64:96, W:W + PIX - 1], flat[:, 1:PIX]).then_inc(s_x3_in[s], 16)

            def load_xq(b, n, s):
                flat = x[b].rearrange("c h w -> c (h w)")
                for q in range(Q):
                    sp.dma_start(xq[s][32 * q:32 * q + 32, :], flat[:, q * QPIX:(q + 1) * QPIX]).then_inc(s_xq_in[s], 16)

            def store_a(b, n, s, more):
                sp.wait_ge(s_x2_ready, NCH * (b + 1))
                for q in range(Q):
                    sp.dma_start(x2_d[b, :, q * QPIX:(q + 1) * QPIX], xq[s][32 * q:32 * q + 32, :]).then_inc(s_x2_out[s], 16)
                if more is not None:
                    load_x3(*more)
                sp.wait_ge(s_xl_ready, b + 1)
                for part, buf in ((0, xh), (1, xl)):
                    for q in range(Q):
                        sp.dma_start(xn_d[b, part, :, 1 + q * (H // Q):1 + (q + 1) * (H // Q), :].rearrange("c h w -> c (h w)"),
                                     buf[32 * q:32 * q + 32, :]).then_inc(s_xn_out, 16)
                if more is not None:
                    sp.wait_ge(s_x2_out[s], 64 * (n + 1))
                    load_xq(*more)

            for s in range(2):
                load_xq(*batch(0, s))
                sp.wait_ge(s_x3_zero, 2)
                load_x3(*batch(0, s))
                sp.dma_start(x3[s][96:128, :], t["support"]).then_inc(s_support_in, 16)
            images = xn_d.rearrange("b g c h w -> (b g c) h w").rearrange("(p e) h w -> p e h w", p=128)
            sp.wait_ge(s_pads_zero, 2)
            for row in (0, H + 1):
                sp.dma_start(images[:, :, row, :], xh[:, 0:NB // 2 * WP].rearrange("p (e w) -> p e w", w=WP)).then_inc(s_xn_out, 16)
            with sp.Fori(0, NB // 2 - 1) as pair:
                for s in range(2):
                    store_a(*batch(pair, s), batch(pair + 1, s))
            for s in range(2):
                store_a(*batch(NB // 2 - 1, s), None)

            sp.wait_ge(s_x2_out[0], 64 * NB // 2)
            sp.wait_ge(s_x2_out[1], 64 * NB // 2)
            sp.wait_ge(s_xn_out, 128 * NB + 32)
            sp.wait_ge(s_xl_ready, NB)
            sp.dma_start(spec[0:9, :], t["spectra"]).then_inc(s_spectra_in, 16)

            def load_xs(b, half):
                for g in range(4):
                    src = xn_d[b, g % 2, :, half * (H // 2):half * (H // 2) + HALF, :].rearrange("c h w -> c (h w)")
                    sp.dma_start(xs[half][32 * g:32 * g + 32, :], src).then_inc(s_xs_in[half], 16)

            def image_rows(base, b, half, jr, s):
                first = (half * 8 + 2 * s + jr) * 8 * W
                return base[b, :, half * (PIX // 2):(half + 1) * (PIX // 2)].rearrange(
                    "c (l r) -> c l r", l=2)[:, :, first - half * (PIX // 2):first - half * (PIX // 2) + 8 * W]

            def load_res(b, half):
                for jr in range(2):
                    for s in range(2):
                        p0 = 64 * jr + 32 * s
                        sp.dma_start(res[p0:p0 + 32, :].rearrange("p (l r) -> p l r", l=2),
                                     image_rows(x2_d, b, half, jr, s)).then_inc(s_res_in, 16)

            def store_res(b, half):
                for jr in range(2):
                    for s in range(2):
                        p0 = 64 * jr + 32 * s
                        sp.dma_start(image_rows(out.rearrange("b c h w -> b c (h w)"), b, half, jr, s),
                                     res[p0:p0 + 32, :].rearrange("p (l r) -> p l r", l=2)).then_inc(s_out_stored, 16)

            load_xs(0, 0)
            load_xs(0, 1)
            load_res(0, 0)

            def unit_dma(u, prev, here, nxt):
                sp.wait_ge(s_v_mm, 8 * u)
                if nxt is not None:
                    load_xs(*nxt)
                sp.wait_ge(s_res_done, 4 * u)
                store_res(*prev)
                sp.wait_ge(s_out_stored, 64 * u)
                if here is not None:
                    load_res(*here)

            with sp.Fori(0, NB - 1) as b:
                unit_dma(2 * b + 1, (b, 0), (b, 1), (b + 1, 0))
                unit_dma(2 * b + 2, (b, 1), (b + 1, 0), (b + 1, 1))
            unit_dma(LAST, (NB - 1, 0), (NB - 1, 1), None)
            unit_dma(LAST + 1, (NB - 1, 1), None, None)
            sp.wait_ge(s_out_stored, 64 * 2 * NB)

        @block.gpsimd
        def _(pool):
            for s in range(2):
                pool.memset(x3[s][0:96, :], 0.0).then_inc(s_x3_zero, 1)
            pool.memset(xh.bitcast(f32), 0.0).then_inc(s_pads_zero, 1)
            pool.memset(xl.bitcast(f32), 0.0).then_inc(s_pads_zero, 1)
            pool.memset(powers, -0.5).then_inc(s_pool_consts, 1)
            pool.memset(ones_row, 1.0).then_inc(s_pool_consts, 1)
            pool.wait_ge(s_pool_consts, 2)

            def root(b, k):
                pool.wait_ge(s_ve[k], b + 1)
                pool.tensor_tensor(tiny[f"rstd{k}"], tiny[f"ve{k}"], powers[:, 0:1], ALU.pow).then_inc(s_rstd[k], 1)
                pool.wait_ge(s_rstd[k], b + 1)

            root(0, 1)
            root(1, 1)
            with pool.Fori(0, NB // 2 - 1) as pair:
                root(2 * pair, 2)
                root(2 * pair + 2, 1)
                root(2 * pair + 1, 2)
                root(2 * pair + 3, 1)
            root(NB - 2, 2)
            root(NB - 1, 2)

            pool.wait_ge(s_xl_ready, NB)
            for s in range(2):
                pool.memset(win[s][:, 16 * WIN:1632].bitcast(f32), 0.0).then_inc(s_win_room, 1)

            pool.wait_ge(s_win_room, 2)

            def roots(u):
                for k in range(4):
                    pool.wait_ge(s_var_eps, 4 * u + k + 1)
                    slot = slice(16 * (k % 2), 16 * (k % 2) + 16)
                    pool.tensor_tensor(tiny["rstd"][:, slot], tiny["var_eps"][:, slot], powers, ALU.pow).then_inc(s_root, 1)
                    pool.wait_ge(s_root, 4 * u + k + 1)

            with pool.Fori(0, 2 * NB) as u:
                roots(u)

        @block.tensor
        def _(pe):
            stats_bank, corr_bank = banks[4], banks[5]

            pe.wait_ge(s_small_in, 16 * len(small))
            pe.wait_ge(s_pool_consts, 2)
            pe.wait_ge(s_prep_qk, 1)
            pe.transpose(banks[6][:, 0:128], prep_qk, ident)
            pe.transpose(banks[6][0:9, 128:256], tiny["dw_qk_s"], ident).then_inc(s_qk_t, 1)
            pe.wait_ge(s_prep_v, 1)
            for tap in range(9):
                dst = banks[7][:, 64 * tap:64 * tap + 64] if tap < 8 else banks[0][:, 0:64]
                last = pe.transpose(dst, prep_v[0:64, 128 * tap:128 * tap + 128], ident[0:64, 0:64])
            last.then_inc(s_v_t, 1)
            pe.wait_ge(s_low_parts, 1)

            def moments(b, k):
                pe.wait_ge(s_mv[k], b + 1)
                pe.matmul(stats_bank[:, 0:1], quarter_mean, tiny[f"mv{k}"][:, 0:1], start=True, stop=True).then_inc(s_mean_mm[k], 1)
                pe.wait_ge(s_varq[k], b + 1)
                pe.matmul(stats_bank[:, 1:2], quarter_mean, tiny[f"varq{k}"], start=True, stop=True).then_inc(s_var_mm[k], 1)

            def weights(b, n, s):
                moments(b, 1)
                pe.wait_ge(s_xnsum, b + 1)
                pe.matmul(stats_bank[:, 2:3], image_mean, tiny["xnsum"], start=True, stop=True).then_inc(s_pooled_mm, 1)
                pe.wait_ge(s_pooled, b + 1)
                pe.matmul(stats_bank[:, 3:4], small["w1"], tiny["pooled"], start=True, stop=True).then_inc(s_hid_mm, 1)
                pe.wait_ge(s_hid_relu, b + 1)
                pe.matmul(stats_bank[0:1, 4:8], tiny["hid_relu"], small["w2"], start=True, stop=True).then_inc(s_logit_mm, 1)
                pe.wait_ge(s_att, b + 1)
                pe.matmul(stats_bank[:, 8:12], ones_row[0:1, :], tiny["att"][0:1, :], start=True, stop=True).then_inc(s_att_mm, 1)
                pe.wait_ge(s_mean_w, b + 1)
                pe.matmul(corr_bank[96:128, 0:96], mean_w[0:96, :], conv_w[s][0:96, :], start=True, stop=False)
                pe.matmul(corr_bank[96:128, 0:96], ident[0:96, 0:32], small["bias_row"][0:96, :], start=False, stop=True).then_inc(s_corr_mm, 1)

            def conv(b, n, s):
                pe.wait_ge(s_conv_w, b + 1)
                pe.wait_ge(s_edges, 2 * (b + 1))
                pe.wait_ge(s_support_in, 32)
                for k in range(NCH):
                    if positive(NCH * b + k - 3):
                        pe.wait_ge(s_x2_ready, NCH * b + k - 3)
                    for q in range(Q):
                        for dy in range(3):
                            row = q * (H // Q) + 4 * k + dy
                            mm = pe.matmul(banks[k % 4][32 * q:32 * q + 32, :], conv_w[s][:, 32 * dy:32 * dy + 32],
                                           x3[s][:, row * W:row * W + 512], start=dy == 0, stop=dy == 2)
                    mm.then_inc(s_conv_mm, 1)

            def slot(b, n, s, after):
                moments(b - 1, 2)
                conv(b, n, s)
                if after is not None:
                    weights(*after)

            weights(*batch(0, 0))
            conv(*batch(0, 0))
            weights(*batch(0, 1))
            with pe.Fori(0, NB // 2 - 1) as pair:
                slot(*batch(pair, 1), batch(pair + 1, 0))
                slot(*batch(pair + 1, 0), batch(pair + 1, 1))
            slot(*batch(NB // 2 - 1, 1), None)
            moments(NB - 1, 2)

            pe.wait_ge(s_spectra_in, 16)
            for m0 in range(0, 192, 8):
                if positive(m0 // 8 - 3):
                    pe.wait_ge(s_g_ready, m0 // 8 - 3)
                for m in range(m0, m0 + 8):
                    chans = dw_t[0:9, 64:128] if m < 128 else dw_t[0:9, 0:64]
                    mm = pe.matmul(banks[m0 // 8 % 4][0:WIN, 64 * (m - m0):64 * (m - m0) + 64],
                                   spec[0:9, WIN * m:WIN * m + WIN], chans, start=True, stop=True)
                mm.then_inc(s_g_mm, 1)
            pe.wait_ge(s_g_ready, 24)
            t_bank, f_bank, i_bank = banks[4], banks[6], banks[7]

            def hidden_group(u, g, ring):
                if g % 4 == 0:
                    pe.wait_ge(s_win_ready, 8 * u + g // 4 + 1)
                if g < 2 and positive(16 * u):
                    pe.wait_ge(s_q_copied, 16 * u)
                if positive(32 * u + g + 1 - ring):
                    pe.wait_ge(s_h_ready, 32 * u + g + 1 - ring)
                w = win[g // 4 % 2]
                for i in range(4):
                    first = (4 * (g % 4) + i) * WIN
                    mm = pe.matmul(banks[g % ring][:, 128 * i:128 * i + 128], w[:, first:first + 128], hidden_w,
                                   start=True, stop=True)
                mm.then_inc(s_hidden_mm, 1)

            def v_chunk(u, half, k, jr, every, between):
                chunk = 2 * k + jr
                if chunk == 1:
                    pe.wait_ge(s_y_ready, 8 * (u + 1))
                if chunk > 2:
                    pe.wait_ge(s_gated, 8 * u + chunk - 2)
                for s in range(2):
                    for tap in range(9):
                        dy, dx = tap // 3, tap % 3
                        row = 8 * (2 * s + jr) + dy
                        mm = pe.matmul(v_banks[chunk % 3][64 * s:64 * s + 64, :], v_w[:, 64 * tap:64 * tap + 64],
                                       at(xs[half], row * WP + 32 * k + dx, [32 * WP, 2], [WP, 8], [1, 32]),
                                       start=tap == 0, stop=tap == 8)
                        if (9 * s + tap) % every == every - 1:
                            between()
                mm.then_inc(s_v_mm, 1)

            def turn(u, k, jr):
                pe.wait_ge(s_y_norm, 4 * u + k + 1)
                if k + jr > 0:
                    pe.wait_ge(s_t_copied, 8 * u + 2 * k + jr)
                for i in range(4):
                    tr = pe.transpose(t_bank[:, 128 * i:128 * i + 128],
                                      at(Y, 8 * k + 4 * jr + i, [32, 128]), ident)
                tr.then_inc(s_turned, 1)

            def project(u, k):
                if k > 0:
                    pe.wait_ge(s_res_done, 4 * u + k)
                for jr in range(2):
                    pe.wait_ge(s_gated, 8 * u + 2 * k + jr + 1)
                    mm = pe.matmul(f_bank[64 * jr:64 * jr + 64, :], small["w_out"], gated[jr], start=True, stop=True)
                mm.then_inc(s_project_mm, 1)

            def front(u, half, tail):
                groups = iter(range(32 if u is not None else 0))

                def hidden(n=1):
                    for g in islice(groups, n):
                        hidden_group(u, g, 4 if tail is None else 3)

                if tail is None:
                    hidden(32)
                    return
                v_half = 1 - half
                v_chunk(tail, v_half, 0, 0, 4, hidden)
                v_chunk(tail, v_half, 0, 1, 4, hidden)
                v_chunk(tail, v_half, 1, 0, 4, hidden)
                hidden(2)
                turn(tail, 0, 0)
                turn(tail, 0, 1)
                hidden(2)
                for k in range(1, 4):
                    v_chunk(tail, v_half, k, 1, 6, hidden)
                    project(tail, k - 1)
                    turn(tail, k, 0)
                    if k < 3:
                        v_chunk(tail, v_half, k + 1, 0, 6, hidden)
                    else:
                        hidden(1)
                    turn(tail, k, 1)

            def spectral(u, tail):
                def inverse(n):
                    pe.wait_ge(s_prod_ready, 16 * u + n + 1)
                    if n % 2 == 0:
                        if positive(8 * u + n // 2):
                            pe.wait_ge(s_y_ready, 8 * u + n // 2)
                    if n == 0 and tail is not None:
                        pe.wait_ge(s_gated, 8 * u)
                    for lam in range(2):
                        mm = pe.matmul(i_bank[64 * lam:64 * lam + 64, 256 * (n % 2):256 * (n % 2) + 256], small["inverse"],
                                       at(prod[n % 2], 64 * lam, [128, 4], [1, 64]), start=True, stop=True)
                    mm.then_inc(s_inverse_mm, 1)

                pe.wait_ge(s_h_ready, 32 * (u + 1))
                for n in range(16):
                    for done, first, bank, free in ((s_q_mm, 0, banks[n % 2], s_q_copied), (s_k_mm, 64, banks[2 + n % 2], s_prod_ready)):
                        if positive(16 * u + n - 1):
                            pe.wait_ge(free, 16 * u + n - 1)
                        for i in range(4):
                            ch = first + 4 * n + i
                            mm = pe.matmul(bank[:, 128 * i:128 * i + 128], G[0:WIN, 128 * ch:128 * ch + 128],
                                           hwin[0:WIN, 128 * ch:128 * ch + 128], start=True, stop=True)
                        mm.then_inc(done, 1)
                    if n == 1 and tail is not None:
                        project(tail, 3)
                    if n > 0:
                        inverse(n - 1)
                inverse(15)

            front(0, 0, None)
            spectral(0, None)
            with pe.Fori(0, NB - 1) as b:
                for half in (1, 0):
                    u = 2 * b + 2 - half
                    front(u, half, u - 1)
                    spectral(u, u - 1)
            front(LAST, 1, LAST - 1)
            spectral(LAST, LAST - 1)
            front(None, 0, LAST)
            project(LAST, 3)

        @block.scalar
        def _(act):
            act.wait_ge(s_qk_t, 1)
            act.activation(hidden_w, banks[6][:, 0:128], ACT.Copy).then_inc(s_hidden_hi, 1)
            act.activation(dw_t[0:9, :], banks[6][0:9, 128:256], ACT.Copy).then_inc(s_dw_t, 1)
            act.wait_ge(s_v_t, 1)
            act.activation(v_w[:, 0:512], banks[7], ACT.Copy)
            act.activation(v_w[:, 512:576], banks[0][:, 0:64], ACT.Copy).then_inc(s_v_hi, 1)

            def weights(b, n, s):
                act.wait_ge(s_shift1, b + 1)
                act.wait_ge(s_xq_in[s], 64 * (n + 1))
                act.activation(xnf, xq[s], ACT.Identity, bias=tiny["shift1"], scale=tiny["rstd1"],
                               accum_out=tiny["xnsum"]).then_inc(s_xnsum, 1)
                act.wait_ge(s_pooled, b + 1)
                act.activation(tiny["gate_exp"], tiny["pooled"], ACT.Exp, scale=-1.0).then_inc(s_gate_exp, 1)
                act.wait_ge(s_neg_max_t, b + 1)
                act.activation(tiny["exps"][0:1, :], stats_psum[0:1, 4:8], ACT.Exp, scale=1.0 / TEMPERATURE,
                               bias=tiny["neg_max_t"][0:1, :], accum_out=tiny["exp_sum"][0:1, :]).then_inc(s_exps, 1)

            def normalise(b, n, s):
                act.wait_ge(s_shift2, b + 1)
                act.wait_ge(s_xn_out, 128 * b + 32)
                rows = lambda a: a.rearrange("p (h w) -> p h w", w=W)
                padded = xh.rearrange("p (h w) -> p h w", w=WP)[:, :, 1:W + 1]
                act.activation(padded, rows(xq[s]), ACT.Identity, bias=tiny["shift2"], scale=tiny["scale2"]).then_inc(s_xh_ready, 1)
                act.wait_ge(s_xnsum, b + 2 if not (isinstance(b, int) and b >= NB - 1) else NB)
                act.activation(xnf, xq[s], ACT.Identity, bias=tiny["shift2"], scale=tiny["scale2"]).then_inc(s_xnf_ready, 1)

            stats_psum = banks[4]
            weights(*batch(0, 0))
            act.wait_ge(s_xn_out, 32)
            weights(*batch(0, 1))
            with act.Fori(0, NB // 2 - 1) as pair:
                for s in range(2):
                    normalise(*batch(pair, s))
                    weights(*batch(pair + 1, s))
            normalise(*batch(NB // 2 - 1, 0))
            normalise(*batch(NB // 2 - 1, 1))

            g_rows = G.rearrange("p (c m) -> p c m", m=128)
            for i in range(24):
                act.wait_ge(s_g_mm, i + 1)
                src = banks[i % 4][0:WIN, :].rearrange("p (m c) -> p c m", m=8)
                if i < 16:
                    act.activation(g_rows[0:WIN, 64:128, 8 * i:8 * i + 8], src, ACT.Copy).then_inc(s_g_ready, 1)
                else:
                    act.activation(g_rows[0:WIN, 0:64, 8 * i - 128:8 * i - 120], src, ACT.Copy)
                    act.activation(g_rows[0:WIN, 0:64, 8 * i - 64:8 * i - 56], src, ACT.Copy).then_inc(s_g_ready, 1)

            h_rows = hwin.rearrange("p (c j) -> p c j", j=128)
            Y_out = Y.rearrange("p (s c j) -> p c s j", s=2, j=32)
            Y_sq = Y.rearrange("p (s c j) -> p s c j", s=2, j=32)

            def windows_out(u, g, ring):
                pr, k = g // 4, g % 4
                first = 64 * (pr // 4) + 32 * (pr // 2 % 2) + 8 * k + 4 * (pr % 2)
                act.wait_ge(s_hidden_mm, 32 * u + g + 1)
                act.activation(h_rows[0:WIN, :, first:first + 4],
                               banks[g % ring][0:WIN, :].rearrange("p (i c) -> p c i", i=4), ACT.Copy).then_inc(s_h_ready, 1)

            def square(u, k):
                act.wait_ge(s_y_centred, 4 * u + k + 1)
                if k > 0:
                    act.wait_ge(s_sq_sums, 4 * u + k)
                act.activation(squares.rearrange("p (s c j) -> p s c j", s=2, j=8), Y_sq[:, :, :, 8 * k:8 * k + 8],
                               ACT.Square).then_inc(s_squared, 1)

            def turned_out(u, k, jr):
                act.wait_ge(s_turned, 8 * u + 2 * k + jr + 1)
                if k > 0:
                    act.wait_ge(s_project_mm, 4 * u + k)
                for lam in range(2):
                    ins = act.activation(at(gated[jr], 256 * lam, [32, 8], [8, 4], [1, 8]),
                                         at(banks[4], 64 * lam, [8, 8], [128, 4], [1, 8]), ACT.Identity,
                                         bias=tiny["v_shift"], scale=tiny["v_scale"])
                ins.then_inc(s_t_copied, 1)

            def front(u, tail):
                groups = iter(range(32 if u is not None else 0))

                def some(n):
                    for g in islice(groups, n):
                        windows_out(u, g, 4 if tail is None else 3)

                if tail is None:
                    some(32)
                    return
                some(4)
                square(tail, 0)
                some(4)
                square(tail, 1)
                some(3)
                square(tail, 2)
                some(3)
                turned_out(tail, 0, 0)
                turned_out(tail, 0, 1)
                some(2)
                square(tail, 3)
                for k in range(1, 4):
                    some(3)
                    turned_out(tail, k, 0)
                    some(3 if k < 3 else 1)
                    turned_out(tail, k, 1)

            def spectral(u):
                for n in range(16):
                    if n % 2 == 1 and n >= 3:
                        inverse_out(u, n // 2 - 1)
                    act.wait_ge(s_q_mm, 16 * u + n + 1)
                    if positive(16 * u + n - 1):
                        act.wait_ge(s_prod_ready, 16 * u + n - 1)
                    act.activation(q_sb[n % 2], banks[n % 2], ACT.Copy).then_inc(s_q_copied, 1)
                inverse_out(u, 7)

            def inverse_out(u, e):
                act.wait_ge(s_inverse_mm, 16 * u + 2 * e + 2)
                act.activation(Y_out[:, 8 * e:8 * e + 8, :, :], banks[7].rearrange("p (c s j) -> p c s j", s=2, j=32),
                               ACT.Copy).then_inc(s_y_ready, 1)

            front(0, None)
            spectral(0)
            with act.Fori(0, NB - 1) as b:
                for half in (1, 0):
                    u = 2 * b + 2 - half
                    front(u, u - 1)
                    spectral(u)
            front(LAST, LAST - 1)
            spectral(LAST)
            front(None, LAST)

        @block.vector
        def _(dve):
            T = tiny
            dve.wait_ge(s_small_in, 16 * len(small))
            dve.wait_ge(s_pads_zero, 2)
            dve.tensor_scalar(T["gammas"], small["gamma"], float(1 / np.sqrt(np.float32(1 + EPS))), None, ALU.mult).then_inc(s_prep, 1)
            dve.wait_ge(s_prep, 1)
            dve.tensor_reduce(T["qk_max"], small["hidden_qk"], X_AXIS, ALU.max, apply_absolute_value=True).then_inc(s_prep, 1)
            dve.wait_ge(s_prep, 2)
            dve.tensor_scalar(T["qk_max"], T["qk_max"], TINY, None, ALU.max).then_inc(s_prep, 1)
            dve.wait_ge(s_prep, 3)
            dve.reciprocal(T["qk_inv"], T["qk_max"]).then_inc(s_prep, 1)
            dve.wait_ge(s_prep, 4)
            dve.tensor_scalar(T["qk_back"], T["qk_max"], 1 / X_SCALE, None, ALU.mult).then_inc(s_prep, 1)
            dve.wait_ge(s_prep, 5)
            for g in range(4):
                dve.tensor_scalar(prep_qk[:, 32 * g:32 * g + 32], small["hidden_qk"], T["qk_inv"], None, ALU.mult).then_inc(s_prep, 1)
                dve.wait_ge(s_prep, 6 + g)
            dve.tensor_scalar(T["dw_qk_s"], small["dw_qk"], T["qk_back"], None, ALU.mult).then_inc(s_prep_qk, 1)
            dve.wait_ge(s_prep_qk, 1)
            dve.tensor_reduce(T["v_max"], small["hidden_v"], X_AXIS, ALU.max, apply_absolute_value=True).then_inc(s_prep, 1)
            dve.wait_ge(s_prep, 10)
            dve.tensor_scalar(T["v_max"], T["v_max"], TINY, None, ALU.max).then_inc(s_prep, 1)
            dve.wait_ge(s_prep, 11)
            dve.reciprocal(T["v_inv"], T["v_max"]).then_inc(s_prep, 1)
            dve.wait_ge(s_prep, 12)
            dve.tensor_reduce(T["d_max"], small["dw_v"], X_AXIS, ALU.max, apply_absolute_value=True).then_inc(s_prep, 1)
            dve.wait_ge(s_prep, 13)
            dve.tensor_scalar(T["d_max"], T["d_max"], TINY, None, ALU.max).then_inc(s_prep, 1)
            dve.wait_ge(s_prep, 14)
            dve.reciprocal(T["d_inv"], T["d_max"]).then_inc(s_prep, 1)
            dve.wait_ge(s_prep, 15)
            dve.tensor_scalar(T["dw_v_n"], small["dw_v"], T["d_inv"], None, ALU.mult).then_inc(s_prep, 1)
            dve.wait_ge(s_prep, 16)
            for tap in range(9):
                for g in range(4):
                    ins = dve.tensor_scalar(prep_v[:, 128 * tap + 32 * g:128 * tap + 32 * g + 32], small["hidden_v"],
                                            T["v_inv"], T["dw_v_n"][:, tap:tap + 1], ALU.mult, ALU.mult)
            ins.then_inc(s_prep_v, 1)
            dve.tensor_scalar(T["v_back"], T["v_max"], T["d_max"], 1 / X_SCALE, ALU.mult, ALU.mult).then_inc(s_prep, 1)
            dve.wait_ge(s_prep, 17)
            dve.tensor_scalar(T["v_scale"], small["norm_w"], T["v_back"], None, ALU.mult)
            dve.tensor_scalar(T["v_shift"], small["norm_b"], T["v_back"], None, ALU.mult).then_inc(s_v_consts, 1)
            dve.wait_ge(s_hidden_hi, 1)
            dve.tensor_tensor(hidden_w[64:128, :], banks[6][64:128, 0:128], hidden_w[64:128, :], ALU.subtract)
            dve.wait_ge(s_v_hi, 1)
            dve.tensor_tensor(v_w[64:128, 0:512], banks[7][64:128, :], v_w[64:128, 0:512], ALU.subtract)
            dve.tensor_tensor(v_w[64:128, 512:576], banks[0][64:128, 0:64], v_w[64:128, 512:576], ALU.subtract).then_inc(s_low_parts, 1)

            stats_bank, corr_bank = banks[4], banks[5]

            def moments(b, k, stats):
                dve.wait_ge(s_st[k], NCH * (b + 1))
                dve.memset(T[f"dev{k}"], 0.0)
                dve.bn_aggr(T[f"mv{k}"], stats).then_inc(s_mv[k], 1)
                dve.wait_ge(s_mv[k], b + 1)
                dve.wait_ge(s_mean_mm[k], b + 1)
                dve.tensor_copy(T[f"mean{k}"], stats_bank[:, 0:1])
                dve.tensor_tensor(T[f"dev{k}"], T[f"mv{k}"][:, 0:1], stats_bank[:, 0:1], ALU.subtract).then_inc(s_dev[k], 1)
                dve.wait_ge(s_dev[k], b + 1)
                dve.scalar_tensor_tensor(T[f"varq{k}"], T[f"dev{k}"], T[f"dev{k}"], T[f"mv{k}"][:, 1:2], ALU.mult, ALU.add).then_inc(s_varq[k], 1)
                dve.wait_ge(s_varq[k], b + 1)
                dve.wait_ge(s_var_mm[k], b + 1)
                dve.tensor_scalar(T[f"ve{k}"], stats_bank[:, 1:2], EPS, None, ALU.add).then_inc(s_ve[k], 1)
                dve.wait_ge(s_ve[k], b + 1)
                dve.wait_ge(s_rstd[k], b + 1)

            def edges(b, n, s):
                dve.wait_ge(s_x3_in[s], 48 * (n + 1))
                dve.memset(at(x3[s][0:32, :], W, [W, H]), 0.0).then_inc(s_edges, 1)
                dve.memset(at(x3[s][64:96, :], 2 * W - 1, [W, H]), 0.0).then_inc(s_edges, 1)

            def weights(b, n, s):
                dve.wait_ge(s_xq_in[s], 64 * (n + 1))
                for k in range(NCH):
                    dve.bn_stats(st1[:, 6 * k:6 * k + 6], xq[s][:, 512 * k:512 * k + 512]).then_inc(s_st[1], 1)
                moments(b, 1, st1)
                dve.scalar_tensor_tensor(T["shift1"], T["mean1"], -1.0, T["rstd1"], ALU.mult, ALU.mult).then_inc(s_shift1, 1)
                dve.wait_ge(s_shift1, b + 1)
                dve.wait_ge(s_pooled_mm, b + 1)
                dve.tensor_copy(T["pooled"], stats_bank[:, 2:3]).then_inc(s_pooled, 1)
                dve.wait_ge(s_hid_mm, b + 1)
                dve.tensor_scalar(T["hid"], stats_bank[:, 3:4], T["gammas"], small["beta"], ALU.mult, ALU.add).then_inc(s_hid, 1)
                dve.wait_ge(s_hid, b + 1)
                dve.tensor_scalar(T["hid_relu"], T["hid"], 0.0, None, ALU.max).then_inc(s_hid_relu, 1)
                dve.wait_ge(s_logit_mm, b + 1)
                dve.tensor_reduce(T["neg_max"][0:1, :], stats_bank[0:1, 4:8], X_AXIS, ALU.max, negate=True).then_inc(s_neg_max, 1)
                dve.wait_ge(s_neg_max, b + 1)
                dve.tensor_scalar(T["neg_max_t"][0:1, :], T["neg_max"][0:1, :], 1.0 / TEMPERATURE, None, ALU.mult).then_inc(s_neg_max_t, 1)
                dve.wait_ge(s_gate_exp, b + 1)
                dve.tensor_scalar(T["gate_den"], T["gate_exp"], 1.0, None, ALU.add).then_inc(s_gate_den, 1)
                dve.wait_ge(s_gate_den, b + 1)
                dve.reciprocal(T["gate"], T["gate_den"]).then_inc(s_gate, 1)
                dve.wait_ge(s_gate, b + 1)
                dve.tensor_scalar(T["chan_scale"], T["gate"], T["rstd1"], None, ALU.mult).then_inc(s_chan_scale, 1)
                dve.wait_ge(s_exps, b + 1)
                dve.reciprocal(T["exp_inv"][0:1, :], T["exp_sum"][0:1, :]).then_inc(s_exp_inv, 1)
                dve.wait_ge(s_exp_inv, b + 1)
                dve.tensor_scalar(T["att"][0:1, :], T["exps"][0:1, :], T["exp_inv"][0:1, :], None, ALU.mult).then_inc(s_att, 1)
                dve.wait_ge(s_att_mm, b + 1)
                dve.tensor_copy(T["att_all"], stats_bank[:, 8:12]).then_inc(s_att_all, 1)
                dve.wait_ge(s_att_all, b + 1)
                agg, dyn = T["agg"][0:96, :], small["dyn_w"][0:96, :]
                dve.tensor_scalar(agg, dyn[:, 0:3], T["att_all"][0:96, 0:1], None, ALU.mult).then_inc(s_agg, 1)
                dve.wait_ge(s_agg, 4 * b + 1)
                for k in range(1, 4):
                    dve.scalar_tensor_tensor(agg, dyn[:, 3 * k:3 * k + 3], T["att_all"][0:96, k:k + 1], agg, ALU.mult, ALU.add).then_inc(s_agg, 1)
                    dve.wait_ge(s_agg, 4 * b + 1 + k)
                dve.wait_ge(s_chan_scale, b + 1)
                for dy in range(3):
                    dve.tensor_scalar(conv_w[s][0:96, 32 * dy:32 * dy + 32], small["conv1"][0:96, :], agg[:, dy:dy + 1],
                                      T["chan_scale"][0:96, :], ALU.mult, ALU.mult)
                dve.tensor_scalar(mean_w, small["tap_group"], T["mean1"], -1.0, ALU.mult, ALU.mult).then_inc(s_mean_w, 1)
                dve.wait_ge(s_corr_mm, b + 1)
                dve.tensor_copy(conv_w[s][96:128, :], corr_bank[96:128, 0:96]).then_inc(s_conv_w, 1)
                edges(b, n, s)

            def conv(b, n, s):
                for k in range(NCH):
                    dve.wait_ge(s_conv_mm, NCH * b + k + 1)
                    piece = xq[s][:, 512 * k:512 * k + 512]
                    dve.tensor_tensor(piece, banks[k % 4], piece, ALU.add).then_inc(s_x2_ready, 1)
                    if k > 0:
                        second_stats(b, s, k - 1)
                second_stats(b, s, NCH - 1)

            def second_stats(b, s, k):
                dve.wait_ge(s_x2_ready, NCH * b + k + 1)
                dve.bn_stats(st2[:, 6 * k:6 * k + 6], xq[s][:, 512 * k:512 * k + 512]).then_inc(s_st[2], 1)

            def normalise(b, n, s):
                moments(b, 2, st2)
                dve.tensor_scalar(T["scale2"], T["rstd2"], X_SCALE, None, ALU.mult).then_inc(s_scale2, 1)
                dve.wait_ge(s_scale2, b + 1)
                dve.scalar_tensor_tensor(T["shift2"], T["mean2"], -1.0, T["scale2"], ALU.mult, ALU.mult).then_inc(s_shift2, 1)

            def low(b):
                dve.wait_ge(s_xnf_ready, b + 1)
                padded = lambda a: a.rearrange("p (h w) -> p h w", w=WP)[:, :, 1:W + 1]
                dve.tensor_tensor(padded(xl), xnf.rearrange("p (h w) -> p h w", w=W), padded(xh), ALU.subtract).then_inc(s_xl_ready, 1)

            weights(*batch(0, 0))
            conv(*batch(0, 0))
            weights(*batch(0, 1))
            with dve.Fori(0, NB // 2 - 1) as pair:
                for prev, here, after in ((batch(pair, 0), batch(pair, 1), batch(pair + 1, 0)),
                                          (batch(pair, 1), batch(pair + 1, 0), batch(pair + 1, 1))):
                    normalise(*prev)
                    low(prev[0])
                    conv(*here)
                    weights(*after)
            normalise(*batch(NB // 2 - 1, 0))
            low(NB - 2)
            conv(*batch(NB // 2 - 1, 1))
            normalise(*batch(NB // 2 - 1, 1))
            low(NB - 1)

            Y4 = Y.rearrange("p (s c j) -> p s c j", s=2, j=32)
            sq4 = squares.rearrange("p (s c j) -> p s c j", s=2, j=8)
            by_chan = lambda a: a.rearrange("p s c j -> p s j c")
            over = lambda a: a.rearrange("p (s j) -> p s j", s=2).unsqueeze(2).broadcast_to([128, 2, 64, 8])
            pair = lambda a: a.rearrange("p (s j) -> p s j", s=2)

            def window(u, half, r, b=None):
                if positive(32 * u + 4 * (r - 1)):
                    dve.wait_ge(s_hidden_mm, 32 * u + 4 * (r - 1))
                if r == 0:
                    dve.wait_ge(s_xs_in[half], 64 * (b + 1))
                dve.tensor_copy(win[r % 2][:, 0:16 * WIN].rearrange("p (j y x) -> p j y x", y=10, x=10),
                                     at(xs[half], 8 * r * WP, [8, 16], [WP, 10], [1, 10])).then_inc(s_win_ready, 1)

            def channel_sums(u, i):
                dve.wait_ge(s_y_ready, 8 * u + 2 * i + 2)
                part = T["neg_mu"] if i == 0 else T["part_sums"]
                dve.tensor_reduce(pair(part), by_chan(Y4[:, :, 16 * i:16 * i + 16, :]), X_AXIS, ALU.add).then_inc(s_part_sums, 1)
                dve.wait_ge(s_part_sums, 4 * u + i + 1)
                if i > 0:
                    dve.tensor_tensor(T["neg_mu"], T["neg_mu"], T["part_sums"], ALU.add).then_inc(s_sums, 1)
                    dve.wait_ge(s_sums, 3 * u + i)

            def negative_mean(u):
                channel_sums(u, 3)
                dve.tensor_scalar(T["neg_mu"], T["neg_mu"], -1.0 / 64, None, ALU.mult).then_inc(s_neg_mu, 1)
                dve.wait_ge(s_neg_mu, u + 1)

            def centre(u, k):
                piece = Y4[:, :, :, 8 * k:8 * k + 8]
                neg_mu = pair(T["neg_mu"])[:, :, 8 * k:8 * k + 8].unsqueeze(2).broadcast_to([128, 2, 64, 8])
                dve.tensor_tensor(piece, piece, neg_mu, ALU.add).then_inc(s_y_centred, 1)

            def variance(u, k):
                dve.wait_ge(s_squared, 4 * u + k + 1)
                slot = slice(16 * (k % 2), 16 * (k % 2) + 16)
                dve.tensor_reduce(pair(T["sq_sums"][:, slot]), by_chan(sq4), X_AXIS, ALU.add).then_inc(s_sq_sums, 1)
                dve.wait_ge(s_sq_sums, 4 * u + k + 1)
                if k > 1:
                    dve.wait_ge(s_root, 4 * u + k - 1)
                dve.tensor_scalar(T["var_eps"][:, slot], T["sq_sums"][:, slot], 1.0 / 64, EPS, ALU.mult, ALU.add).then_inc(s_var_eps, 1)

            def scale(u, k):
                piece = Y4[:, :, :, 8 * k:8 * k + 8]
                dve.wait_ge(s_root, 4 * u + k + 1)
                dve.wait_ge(s_y_centred, 4 * u + k + 1)
                slot = slice(16 * (k % 2), 16 * (k % 2) + 16)
                dve.tensor_tensor(piece, piece, over(T["rstd"][:, slot]), ALU.mult).then_inc(s_y_norm, 1)

            def gate(u, k, jr):
                dve.wait_ge(s_t_copied, 8 * u + 2 * k + jr + 1)
                dve.wait_ge(s_v_mm, 8 * u + 2 * k + jr + 1)
                dve.tensor_tensor(gated[jr], gated[jr], v_banks[(2 * k + jr) % 3], ALU.mult).then_inc(s_gated, 1)

            def residual(u, k):
                dve.wait_ge(s_project_mm, 4 * u + k + 1)
                if k == 0:
                    dve.wait_ge(s_res_in, 64 * (u + 1))
                piece = at(res, 32 * k, [1024, 2], [W, 8], [1, 32])
                dve.tensor_tensor(piece, banks[6].rearrange("p (l r w) -> p l r w", l=2, r=8), piece, ALU.add).then_inc(s_res_done, 1)

            def front(u, half, tail):
                rows = iter(range(2, 8) if u is not None else ())

                def windows(n=1):
                    for r in islice(rows, n):
                        window(u, half, r)

                if tail is None:
                    windows(6)
                    return
                negative_mean(tail)
                centre(tail, 0)
                centre(tail, 1)
                windows()
                variance(tail, 0)
                centre(tail, 2)
                windows()
                variance(tail, 1)
                scale(tail, 0)
                windows()
                centre(tail, 3)
                gate(tail, 0, 0)
                gate(tail, 0, 1)
                variance(tail, 2)
                scale(tail, 1)
                windows()
                variance(tail, 3)
                scale(tail, 2)
                for k in range(1, 4):
                    gate(tail, k, 0)
                    residual(tail, k - 1)
                    windows()
                    gate(tail, k, 1)
                    if k == 1:
                        scale(tail, 3)

            def spectral(u, tail, nxt):
                for n in range(16):
                    dve.wait_ge(s_q_copied, 16 * u + n + 1)
                    dve.wait_ge(s_k_mm, 16 * u + n + 1)
                    if positive(16 * u + n - 1):
                        dve.wait_ge(s_inverse_mm, 16 * u + n - 1)
                    dve.tensor_tensor(prod[n % 2], banks[2 + n % 2], q_sb[n % 2], ALU.mult).then_inc(s_prod_ready, 1)
                    if n == 1 and tail is not None:
                        residual(tail, 3)
                    if nxt is not None and n in (8, 11):
                        window(nxt[0], nxt[1], (n - 8) // 3, nxt[2])
                    if n in (6, 10, 14):
                        channel_sums(u, (n - 6) // 4)

            dve.wait_ge(s_g_ready, 24)
            dve.wait_ge(s_win_room, 2)
            window(0, 0, 0, 0)
            window(0, 0, 1, 0)
            front(0, 0, None)
            spectral(0, None, (1, 1, 0))
            with dve.Fori(0, NB - 1) as b:
                for half in (1, 0):
                    u = 2 * b + 2 - half
                    front(u, half, u - 1)
                    spectral(u, u - 1, (u + 1, 1 - half, b + 1))
            front(LAST, 1, LAST - 1)
            spectral(LAST, LAST - 1, None)
            front(None, 0, LAST)
            residual(LAST, 3)


def kernel(**inputs):
    import concourse.bacc as bacc
    from concourse.bass_utils import run_bass_kernel_spmd

    a = {n: np.asarray(v) for n, v in inputs.items()}

    def padded(v, rows):
        return np.pad(v, ((0, rows - v.shape[0]), (0, 0)))

    def column(v):
        return v.reshape(-1, 1)

    hidden, dw = a["L1_conv_w_hidden"], a["L1_conv_w_dw"].reshape(192, 9)
    w_out = a["L1_conv_w_out"].T
    zero = np.zeros_like(w_out)
    dyn = a["L0_conv_weight"].reshape(4, 32, 3, 3)
    bias_row = np.zeros((96, 96), np.float32)
    bias_row[3, 32:64] = a["L0_conv_conv1_b"]
    arrays = {
        "x": a["x"],
        "w1": np.pad(a["L0_conv_att_w1"].T, ((0, 96), (0, 111))),
        "w2": padded(a["L0_conv_att_w2"].T, 128),
        "dyn_w": dyn.transpose(3, 1, 0, 2).reshape(96, 12),
        "conv1": np.tile(a["L0_conv_conv1_w"].T, (3, 1)),
        "bias_row": bias_row,
        "gamma": padded(column(a["L0_conv_bn_gamma"]), 128),
        "beta": padded(column(a["L0_conv_bn_beta"]), 128),
        "hidden_qk": hidden[0:128], "dw_qk": dw[0:128],
        "hidden_v": np.tile(hidden[128:], (2, 1)), "dw_v": np.tile(dw[128:], (2, 1)),
        "norm_w": np.tile(column(a["L1_conv_norm_w"]), (2, 1)), "norm_b": np.tile(column(a["L1_conv_norm_b"]), (2, 1)),
        "w_out": np.block([[w_out, zero], [zero, w_out]]),
        **constants(),
    }
    arrays = {n: np.ascontiguousarray(v) for n, v in arrays.items()}
    nc = bacc.Bacc("TRN2", target_bir_lowering=False, num_devices=1)
    t = {n: nc.dram_tensor(f"{n}_in", v.shape, mybir.dt.from_np(v.dtype), kind="ExternalInput").ap() for n, v in arrays.items()}
    out = nc.dram_tensor("out", a["x"].shape, mybir.dt.float32, kind="ExternalOutput").ap()
    build(nc, t, out)
    r = run_bass_kernel_spmd(nc, [{f"{n}_in": v for n, v in arrays.items()}], core_ids=[0])
    return r.results[0]["out"]
```

```python
from contextlib import ExitStack
from itertools import islice

import numpy as np

import concourse.bass as bass
from concourse import mybir

EPS = 1e-5
TEMPERATURE = 30.0
X_SCALE = 256.0
TINY = 1e-30

TABLES = {"tables": (("identity", 128), ("inverse", 64), ("w_out", 64)),
          "weights": (("quarter_mean", 128), ("tap_group", 32), ("w1", 128), ("w2", 4), ("dyn_w", 12), ("conv1", 32),
                      ("bias_row", 96), ("gamma", 1), ("beta", 1), ("hidden_qk", 32), ("dw_qk", 9), ("hidden_v", 32),
                      ("dw_v", 9), ("norm_w", 1), ("norm_b", 1))}


def constants():
    p = np.arange(128)
    same_channel = (p[:, None] % 32 == p[None, :] % 32).astype(np.float32)
    out = {"identity": np.eye(128, dtype=np.float32), "quarter_mean": same_channel / 4}
    group = np.zeros((128, 32), np.float32)
    for g in range(3):
        group[32 * g:32 * g + 32, g] = 1
    out["tap_group"] = group
    support = np.zeros((4, 130, 128), np.float32)
    support[0, 1:129, 1:] = 1
    support[1, 1:129, :] = 1
    support[2, 1:129, :127] = 1
    support[3] = 1
    out["support"] = support.reshape(4, 130 * 128)
    u, v = np.meshgrid(np.arange(8), np.arange(8), indexing="ij")
    u, v = u.ravel(), v.ravel()
    spectra = np.zeros((9, 3, 64, 10, 10), np.float64)
    for dy in range(3):
        for dx in range(3):
            for y in range(8):
                for x in range(8):
                    a = 2 * np.pi * ((u * y + v * x) % 8) / 8
                    spectra[3 * dy + dx, :, :, y + dy, x + dx] = [np.cos(a), np.sin(a), np.cos(a) + np.sin(a)]
    spectra = np.pad(spectra.reshape(9, 24, 8, 100), ((0, 0), (0, 0), (0, 0), (0, 28)))
    out["spectra"] = np.pad(spectra.transpose(2, 0, 1, 3).reshape(72, 24 * 128), ((0, 24), (0, 0))).astype(np.float32)
    row, tap = np.divmod(np.arange(72), 9)
    out["tap_rows"] = np.pad((tap == np.arange(9)[:, None]).astype(np.float32), ((0, 0), (0, 56)))
    out["row_mask"] = np.pad(np.repeat(row[:, None] == np.arange(8), 64, axis=1), ((0, 24), (0, 0))).astype(np.float32)
    a = 2 * np.pi * ((u[:, None] * u[None, :] + v[:, None] * v[None, :]) % 8) / 8
    out["inverse"] = (np.concatenate([np.cos(a) + np.sin(a), np.sin(a) - np.cos(a)]) / 64).astype(np.float32)
    return out


def build(nc, t, out):
    f32, f16 = mybir.dt.float32, mybir.dt.float16
    ALU, ACT, X_AXIS = mybir.AluOpType, mybir.ActivationFunctionType, mybir.AxisListType.X
    x = t["x"]
    NB, C, H, W = x.shape
    PIX = H * W
    Q = 4
    QPIX = PIX // Q
    NCH = QPIX // 512
    WP = W + 2
    HALF = H // 2 + 2
    WIN = 100
    LAST = 2 * NB - 1

    def dram(name, shape, dt):
        return nc.dram_tensor(name, shape, dt, kind="Internal").ap()

    x2_d = dram("x2_d", [NB, C, PIX], f32)
    xn_d = dram("xn_d", [NB, 2, C, H + 2, WP], f16)

    ctx = ExitStack()
    with ctx:
        def sb(name, cols, dt=f32, rows=128):
            return ctx.enter_context(nc.sbuf_tensor(name, [rows, cols], dt))[:, :]

        banks = [ctx.enter_context(nc.psum_tensor(f"bank{i}", [128, 512], f32))[:, :] for i in range(8)]
        def semaphore(name):
            return ctx.enter_context(nc.semaphore(name))

        def positive(value):
            return not isinstance(value, int) or value > 0

        s_small_in = semaphore("small_in")
        s_support_in = [semaphore(f"support_in{s}") for s in range(2)]
        s_x3_mid_in = [semaphore(f"x3_mid_in{s}") for s in range(2)]
        s_x3_left_in = [semaphore(f"x3_left_in{s}") for s in range(2)]
        s_xr_in = semaphore("xr_in")
        s_x2_out = [semaphore(f"x2_out{s}") for s in range(2)]
        s_xn_out = semaphore("xn_out")
        s_transforms_in = semaphore("transforms_in")
        s_xs_in = [semaphore(f"xs_in{s}") for s in range(2)]
        s_res_in = semaphore("res_in")
        s_out_stored = semaphore("out_stored")
        s_x3_zero = [semaphore(f"x3_zero{s}") for s in range(2)]
        s_pads_zero = semaphore("pads_zero")
        s_pool_consts = semaphore("pool_consts")
        s_win_room = semaphore("win_room")
        s_hwin_zero = semaphore("hwin_zero")
        s_prep = semaphore("prep")
        s_prep_qk = semaphore("prep_qk")
        s_prep_v = semaphore("prep_v")
        s_qk_t = semaphore("qk_t")
        s_v_t = semaphore("v_t")
        s_hidden_hi = semaphore("hidden_hi")
        s_v_hi = semaphore("v_hi")
        s_low_parts = semaphore("low_parts")
        s_taps_mm = semaphore("taps_mm")
        s_taps = semaphore("taps")
        s_g_mm = semaphore("g_mm")
        s_g_ready = semaphore("g_ready")
        s_st = {k: semaphore(f"st{k}") for k in (1, 2)}
        s_mv = {k: semaphore(f"mv{k}") for k in (1, 2)}
        s_mean_mm = {k: semaphore(f"mean_mm{k}") for k in (1, 2)}
        s_dev = {k: semaphore(f"dev{k}") for k in (1, 2)}
        s_varq = {k: semaphore(f"varq{k}") for k in (1, 2)}
        s_var_mm = {k: semaphore(f"var_mm{k}") for k in (1, 2)}
        s_ve = {k: semaphore(f"ve{k}") for k in (1, 2)}
        s_rstd = {k: semaphore(f"rstd{k}") for k in (1, 2)}
        s_shift1 = semaphore("shift1")
        s_quarter_xn = semaphore("quarter_xn")
        s_pooled_mm = semaphore("pooled_mm")
        s_pooled = semaphore("pooled")
        s_hid_mm = semaphore("hid_mm")
        s_hid = semaphore("hid")
        s_hid_relu = semaphore("hid_relu")
        s_logit_mm = semaphore("logit_mm")
        s_neg_max = semaphore("neg_max")
        s_neg_max_t = semaphore("neg_max_t")
        s_gate_exp = semaphore("gate_exp")
        s_gate_den = semaphore("gate_den")
        s_gate = semaphore("gate")
        s_chan_scale = semaphore("chan_scale")
        s_exps = semaphore("exps")
        s_exp_inv = semaphore("exp_inv")
        s_att = semaphore("att")
        s_att_mm = semaphore("att_mm")
        s_att_all = semaphore("att_all")
        s_agg = semaphore("agg")
        s_mean_w = semaphore("mean_w")
        s_corr_mm = semaphore("corr_mm")
        s_conv_w = semaphore("conv_w")
        s_edges = semaphore("edges")
        s_right_act = semaphore("right_act")
        s_right_dve = semaphore("right_dve")
        s_conv_mm = semaphore("conv_mm")
        s_x2_ready = semaphore("x2_ready")
        s_scale2 = semaphore("scale2")
        s_shift2 = semaphore("shift2")
        s_xh_ready = semaphore("xh_ready")
        s_x2n_ready = semaphore("x2n_ready")
        s_xl_ready = semaphore("xl_ready")
        s_win_ready = semaphore("win_ready")
        s_hidden_mm = semaphore("hidden_mm")
        s_h_ready = semaphore("h_ready")
        s_q_mm = semaphore("q_mm")
        s_q_copied = semaphore("q_copied")
        s_k_mm = semaphore("k_mm")
        s_prod_ready = semaphore("prod_ready")
        s_inverse_mm = semaphore("inverse_mm")
        s_y_ready = semaphore("y_ready")
        s_part_sums = semaphore("part_sums")
        s_sums = semaphore("sums")
        s_neg_mu = semaphore("neg_mu")
        s_y_centred = semaphore("y_centred")
        s_squared = semaphore("squared")
        s_sq_sums = semaphore("sq_sums")
        s_var_eps = semaphore("var_eps")
        s_root = semaphore("root")
        s_y_norm = semaphore("y_norm")
        s_turned = semaphore("turned")
        s_t_copied = semaphore("t_copied")
        s_v_mm = semaphore("v_mm")
        s_gated = semaphore("gated")
        s_project_mm = semaphore("project_mm")
        s_res_done = semaphore("res_done")

        def at(ap, offset, *dims):
            return bass.AP(tensor=ap.tensor, offset=ap.offset + offset, ap=[ap.ap[0]] + [list(d) for d in dims])

        v_banks = [banks[5], banks[7], banks[3]]
        taps_banks = [banks[5], banks[7]]

        WORDS = 53200
        arena = sb("arena", WORDS)
        top = [0]

        def take(cols, dt=f32):
            words = cols if dt == f32 else (cols + 1) // 2
            a = arena[:, top[0]:top[0] + words]
            top[0] += words
            assert top[0] <= WORDS, top[0]
            return a if dt == f32 else a.bitcast(dt)

        def take_tables(name):
            pack, first = take(t[name].shape[1]), 0
            for n, cols in TABLES[name]:
                small[n] = pack[:, first:first + cols]
                first += cols
            return pack

        small = {}
        packs = {"tables": take_tables("tables")}
        ident = small["identity"]
        hidden_w = take(128, f16)
        v_w = take(9 * 64, f16)
        dw_t = take(128)
        powers = take(8)
        tiny = {n: take(c) for n, c in (("v_scale", 1), ("v_shift", 1), ("part_sums", 64), ("neg_mu", 64),
                                        ("sq_sums", 16), ("var_eps", 16), ("rstd", 16))}
        phases = top[0]

        x3 = [take((H + 2) * W) for _ in range(2)]
        xr = take(QPIX)
        x2 = [take(QPIX) for _ in range(2)]
        xh, xl = take(QPIX // W * WP, f16), take(QPIX // W * WP, f16)
        prep_qk, prep_v = x2[1][:, 0:128], x2[1][:, 128:128 + 9 * 128]
        packs["weights"] = take_tables("weights")
        quarter_mean = small["quarter_mean"]
        ones_row = take(128)
        conv_w = [take(96) for s in range(2)]
        mean_w = take(32)
        st1, st2 = take(6 * NCH), take(6 * NCH)
        tiny |= {n: take(c) for n, c in (
            ("mv1", 2), ("mean1", 1), ("dev1", 1), ("varq1", 1), ("ve1", 1), ("rstd1", 1), ("shift1", 1),
            ("mv2", 2), ("mean2", 1), ("dev2", 1), ("varq2", 1), ("ve2", 1), ("rstd2", 1), ("scale2", 1), ("shift2", 1),
            ("quarter_xn", 1), ("pooled", 1), ("hid", 1), ("hid_relu", 1), ("neg_max", 1), ("neg_max_t", 1), ("exps", 4),
            ("exp_sum", 1), ("exp_inv", 1), ("att", 4), ("att_all", 4), ("gate_exp", 1), ("gate_den", 1), ("gate", 1),
            ("chan_scale", 1), ("agg", 3), ("gammas", 1), ("qk_max", 1), ("qk_inv", 1), ("qk_back", 1),
            ("v_max", 1), ("v_inv", 1), ("d_max", 1), ("d_inv", 1), ("v_back", 1), ("dw_qk_s", 9), ("dw_v_n", 9))}

        top[0] = phases
        hwin = take(128 * 128)
        Y = take(64 * 64)
        spectra = arena[:, phases:phases + 3072]
        row_mask = arena[:, phases + 3072:phases + 3584]
        taps = [arena[:, phases + 3584 + 512 * i:phases + 4096 + 512 * i] for i in range(2)]
        tap_rows = arena[:, phases + 4608:phases + 4736]
        G_q = take(64 * 64)
        G_k = take(64 * 128)
        squares = take(1024)
        q_sb = [take(512) for _ in range(4)]
        prod = [take(512) for _ in range(2)]
        xs = [take(HALF * WP, f16) for _ in range(2)]
        gated = [take(512) for _ in range(2)]
        res = take(2048)
        top[0] = WORDS - 1632
        win = [take(1632, f16) for _ in range(2)]
        block = ctx.enter_context(nc.Block())

        def right_shift(s, i):
            first, rows = (1 + 16 * i) * W, 16
            return (at(x3[s][0:32, :], first + 1, [W, rows], [1, W - 1]), at(x3[s][32:64, :], first, [W, rows], [1, W - 1]))

        def slots(engine, slot):
            def batch(b):
                return (b, b // 2, b % 2) if 0 <= b < NB else None

            for b in range(-1, 2):
                slot(batch(b - 2), batch(b - 1), batch(b), batch(b + 1))
            with engine.Fori(1, NB // 2 - 1) as pair:
                for odd in range(2):
                    slot((2 * pair + odd - 2, pair - 1, odd), (2 * pair + odd - 1, pair + odd - 1, 1 - odd),
                         (2 * pair + odd, pair, odd), (2 * pair + odd + 1, pair + odd, 1 - odd))
            for b in range(NB - 2, NB + 2):
                slot(batch(b - 2), batch(b - 1), batch(b), batch(b + 1))

        @block.sync
        def _(sp):
            def load_middle(b, n, s):
                sp.dma_start(x3[s][32:64, W:W + PIX], x[b].rearrange("c h w -> c (h w)")).then_inc(s_x3_mid_in[s], 16)

            def load_left(b, n, s):
                sp.dma_start(x3[s][64:96, W:W + PIX - 1], x[b].rearrange("c h w -> c (h w)")[:, 1:PIX]).then_inc(s_x3_left_in[s], 16)

            def store_xn(b):
                sp.wait_ge(s_xl_ready, 4 * (b + 1))
                for part, buf in ((0, xh), (1, xl)):
                    for q in range(Q):
                        sp.dma_start(xn_d[b, part, :, 1 + q * (H // Q):1 + (q + 1) * (H // Q), :].rearrange("c h w -> c (h w)"),
                                     buf[32 * q:32 * q + 32, :]).then_inc(s_xn_out, 16)

            def load_xr(b):
                flat = x[b].rearrange("c h w -> c (h w)")
                for q in range(Q):
                    sp.dma_start(xr[32 * q:32 * q + 32, :], flat[:, q * QPIX:(q + 1) * QPIX]).then_inc(s_xr_in, 16)

            def load_transforms():
                for buf, name in ((spectra, "spectra"), (row_mask, "row_mask"), (tap_rows, "tap_rows")):
                    rows, cols = t[name].shape
                    sp.dma_start(buf[0:rows, 0:cols], t[name]).then_inc(s_transforms_in, 16)

            def load_xs(b, half):
                for g in range(4):
                    src = xn_d[b, g % 2, :, half * (H // 2):half * (H // 2) + HALF, :].rearrange("c h w -> c (h w)")
                    sp.dma_start(xs[half][32 * g:32 * g + 32, :], src).then_inc(s_xs_in[half], 16)

            def load_first_half():
                sp.wait_ge(s_x2_out[0], 64 * NB // 2)
                sp.wait_ge(s_xn_out, 128 * (NB - 1) + 32)
                load_xs(0, 0)

            def slot_dma(older, prev, here, after):
                if prev is not None:
                    b, n, s = prev
                    if after is not None:
                        sp.wait_ge(s_conv_mm, NCH * (b + 1))
                        load_middle(*after)
                    sp.wait_ge(s_x2_ready, NCH * (b + 1))
                    for q in range(Q):
                        sp.dma_start(x2_d[b, :, q * QPIX:(q + 1) * QPIX], x2[s][32 * q:32 * q + 32, :]).then_inc(s_x2_out[s], 16)
                if older is not None:
                    store_xn(older[0])
                if prev is not None:
                    if after is not None:
                        load_left(*after)
                    elif here is not None:
                        load_transforms()
                    else:
                        load_first_half()
                elif after is not None:
                    b, n, s = after
                    load_middle(*after)
                    load_left(*after)
                    sp.wait_ge(s_x3_zero[s], 4)
                    sp.dma_start(x3[s][96:100, :], t["support"]).then_inc(s_support_in[s], 16)
                if after is not None and not (isinstance(after[0], int) and after[0] == NB - 1):
                    sp.wait_ge(s_st[1], NCH * (after[0] + 1))
                    load_xr(after[0] + 1)

            for name, pack in packs.items():
                sp.dma_start(pack, t[name]).then_inc(s_small_in, 16)
            load_xr(0)
            images = xn_d.rearrange("b g c h w -> (b g c) h w").rearrange("(p e) h w -> p e h w", p=128)
            sp.wait_ge(s_pads_zero, 2)
            for row in (0, H + 1):
                sp.dma_start(images[:, :, row, :], xh[:, 0:NB // 2 * WP].rearrange("p (e w) -> p e w", w=WP)).then_inc(s_xn_out, 16)
            slots(sp, slot_dma)

            def image_rows(base, b, half, jr, s):
                first = (half * 8 + 2 * s + jr) * 8 * W
                return base[b, :, half * (PIX // 2):(half + 1) * (PIX // 2)].rearrange(
                    "c (l r) -> c l r", l=2)[:, :, first - half * (PIX // 2):first - half * (PIX // 2) + 8 * W]

            def load_res(b, half):
                for jr in range(2):
                    for s in range(2):
                        p0 = 64 * jr + 32 * s
                        sp.dma_start(res[p0:p0 + 32, :].rearrange("p (l r) -> p l r", l=2),
                                     image_rows(x2_d, b, half, jr, s)).then_inc(s_res_in, 16)

            def store_res(b, half):
                for jr in range(2):
                    for s in range(2):
                        p0 = 64 * jr + 32 * s
                        sp.dma_start(image_rows(out.rearrange("b c h w -> b c (h w)"), b, half, jr, s),
                                     res[p0:p0 + 32, :].rearrange("p (l r) -> p l r", l=2)).then_inc(s_out_stored, 16)

            sp.wait_ge(s_x2_out[1], 64 * NB // 2)
            load_xs(0, 1)
            sp.wait_ge(s_xn_out, 128 * NB + 32)
            load_res(0, 0)

            def unit_dma(u, prev, here, nxt):
                sp.wait_ge(s_v_mm, 8 * u)
                if nxt is not None:
                    load_xs(*nxt)
                sp.wait_ge(s_res_done, 4 * u)
                store_res(*prev)
                sp.wait_ge(s_out_stored, 64 * u)
                if here is not None:
                    load_res(*here)

            with sp.Fori(0, NB - 1) as b:
                unit_dma(2 * b + 1, (b, 0), (b, 1), (b + 1, 0))
                unit_dma(2 * b + 2, (b, 1), (b + 1, 0), (b + 1, 1))
            unit_dma(LAST, (NB - 1, 0), (NB - 1, 1), None)
            unit_dma(LAST + 1, (NB - 1, 1), None, None)
            sp.wait_ge(s_out_stored, 64 * 2 * NB)

        @block.gpsimd
        def _(pool):
            pool.memset(powers, -0.5).then_inc(s_pool_consts, 1)
            pool.memset(ones_row, 1.0).then_inc(s_pool_consts, 1)
            pool.memset(xh.bitcast(f32), 0.0).then_inc(s_pads_zero, 1)
            pool.memset(xl.bitcast(f32), 0.0).then_inc(s_pads_zero, 1)
            pool.wait_ge(s_pool_consts, 2)
            pool.wait_ge(s_pads_zero, 2)

            def clear(s):
                for i, row in enumerate((0, H + 1)):
                    pool.memset(x3[s][0:96, row * W:row * W + W], 0.0).then_inc(s_x3_zero[s], 1)
                    pool.wait_ge(s_x3_zero[s], i + 1)
                pool.memset(at(x3[s][0:32, :], W, [W, H]), 0.0).then_inc(s_x3_zero[s], 1)
                pool.wait_ge(s_x3_zero[s], 3)
                pool.memset(x3[s][96:128, :], 0.0).then_inc(s_x3_zero[s], 1)
                pool.wait_ge(s_x3_zero[s], 4)

            clear(0)

            def root(b, k):
                pool.wait_ge(s_ve[k], b + 1)
                pool.tensor_tensor(tiny[f"rstd{k}"], tiny[f"ve{k}"], powers[:, 0:1], ALU.pow).then_inc(s_rstd[k], 1)
                pool.wait_ge(s_rstd[k], b + 1)

            def slot_roots(older, prev, here, after):
                if prev is not None:
                    root(prev[0], 2)
                if after is not None:
                    root(after[0], 1)
                    if prev is None and here is None:
                        clear(1)
                elif here is not None:
                    pool.wait_ge(s_x2_ready, NCH * (NB - 1))
                    pool.memset(hwin[96:128, 0:64 * 128], 0.0).then_inc(s_hwin_zero, 1)
                    pool.wait_ge(s_hwin_zero, 1)

            slots(pool, slot_roots)

            pool.wait_ge(s_xl_ready, 4 * NB)
            for s in range(2):
                pool.memset(win[s][:, 16 * WIN:1632].bitcast(f32), 0.0).then_inc(s_win_room, 1)

            pool.wait_ge(s_win_room, 2)

            def roots(u):
                for p in range(8):
                    pool.wait_ge(s_var_eps, 8 * u + p + 1)
                    slot = slice(8 * (p % 2), 8 * (p % 2) + 8)
                    pool.tensor_tensor(tiny["rstd"][:, slot], tiny["var_eps"][:, slot], powers, ALU.pow).then_inc(s_root, 1)
                    pool.wait_ge(s_root, 8 * u + p + 1)

            with pool.Fori(0, 2 * NB) as u:
                roots(u)

        @block.tensor
        def _(pe):
            stats_bank, corr_bank, norm_bank = banks[4], banks[5], banks[6]

            pe.wait_ge(s_small_in, 16 * len(packs))
            pe.wait_ge(s_pool_consts, 2)
            pe.wait_ge(s_prep_qk, 1)
            pe.transpose(banks[6][:, 0:128], prep_qk, ident)
            pe.transpose(banks[6][0:9, 128:256], tiny["dw_qk_s"], ident).then_inc(s_qk_t, 1)
            pe.wait_ge(s_prep_v, 1)
            for tap in range(9):
                dst = banks[7][:, 64 * tap:64 * tap + 64] if tap < 8 else banks[0][:, 0:64]
                last = pe.transpose(dst, prep_v[0:64, 128 * tap:128 * tap + 128], ident[0:64, 0:64])
            last.then_inc(s_v_t, 1)
            pe.wait_ge(s_low_parts, 1)

            def beside(prev, after, at):
                if prev is not None:
                    b = prev[0]
                    if at == 8:
                        pe.wait_ge(s_mv[2], b + 1)
                        pe.matmul(norm_bank[:, 0:1], quarter_mean, tiny["mv2"][:, 0:1], start=True, stop=True).then_inc(s_mean_mm[2], 1)
                    if at == 14:
                        pe.wait_ge(s_varq[2], b + 1)
                        pe.matmul(norm_bank[:, 1:2], quarter_mean, tiny["varq2"], start=True, stop=True).then_inc(s_var_mm[2], 1)
                if after is not None:
                    b, n, s = after
                    if at == 13:
                        pe.wait_ge(s_mv[1], b + 1)
                        pe.matmul(stats_bank[:, 0:1], quarter_mean, tiny["mv1"][:, 0:1], start=True, stop=True).then_inc(s_mean_mm[1], 1)
                    if at == 16:
                        pe.wait_ge(s_varq[1], b + 1)
                        pe.matmul(stats_bank[:, 1:2], quarter_mean, tiny["varq1"], start=True, stop=True).then_inc(s_var_mm[1], 1)
                    if at == 19:
                        pe.wait_ge(s_quarter_xn, b + 1)
                        pe.matmul(stats_bank[:, 2:3], quarter_mean, tiny["quarter_xn"], start=True, stop=True).then_inc(s_pooled_mm, 1)
                    if at == 20:
                        pe.wait_ge(s_pooled, b + 1)
                        pe.matmul(stats_bank[:, 3:4], small["w1"], tiny["pooled"], start=True, stop=True).then_inc(s_hid_mm, 1)
                    if at == 22:
                        pe.wait_ge(s_hid_relu, b + 1)
                        pe.matmul(stats_bank[0:1, 4:8], tiny["hid_relu"], small["w2"], start=True, stop=True).then_inc(s_logit_mm, 1)
                    if at == 25:
                        pe.wait_ge(s_att, b + 1)
                        pe.matmul(stats_bank[:, 8:12], ones_row[0:1, :], tiny["att"][0:1, :], start=True, stop=True).then_inc(s_att_mm, 1)
                    if at == 29:
                        pe.wait_ge(s_mean_w, b + 1)
                        pe.matmul(corr_bank[96:128, 0:96], mean_w[0:96, :], conv_w[s][0:96, :], start=True, stop=False)
                        pe.matmul(corr_bank[96:128, 0:96], ident[0:96, 0:32], small["bias_row"][0:96, :], start=False, stop=True).then_inc(s_corr_mm, 1)

            def slot(older, prev, here, after):
                if here is not None:
                    b, n, s = here
                    pe.wait_ge(s_conv_w, b + 1)
                    pe.wait_ge(s_edges, b + 1)
                    pe.wait_ge(s_right_act, 5 * (b + 1))
                    pe.wait_ge(s_right_dve, 3 * (b + 1))
                    pe.wait_ge(s_support_in[s], 16)
                for k in range(NCH):
                    if here is not None and positive(NCH * b + k - 3):
                        pe.wait_ge(s_x2_ready, NCH * b + k - 3)
                    for q in range(Q):
                        beside(prev, after, Q * k + q)
                        if here is None:
                            continue
                        for dy in range(3):
                            row = q * (H // Q) + 4 * k + dy
                            mm = pe.matmul(banks[k % 4][32 * q:32 * q + 32, :], conv_w[s][:, 32 * dy:32 * dy + 32],
                                           x3[s][:, row * W:row * W + 512], start=dy == 0, stop=dy == 2)
                    if here is not None:
                        mm.then_inc(s_conv_mm, 1)
                    if here is None and prev is not None and k == 2:
                        pe.wait_ge(s_transforms_in, 48)
                        for i, chans in enumerate((dw_t[0:9, 64:128], dw_t[0:9, 0:64])):
                            pe.matmul(taps_banks[i][0:96, :].rearrange("p (m c) -> p m c", m=8), tap_rows[0:9, 0:96],
                                      chans.unsqueeze(1).broadcast_to([9, 8, 64]), start=True, stop=True).then_inc(s_taps_mm, 1)

            slots(pe, slot)

            pe.wait_ge(s_x2_ready, NCH * NB)
            for m in range(24):
                if m % 16 == 0:
                    pe.wait_ge(s_taps, m // 16 + 1)
                if m > 3:
                    pe.wait_ge(s_g_ready, m - 3)
                pe.matmul(banks[m % 4], spectra[0:96, 128 * m:128 * m + 128], taps[m // 16][0:96, :],
                          start=True, stop=True).then_inc(s_g_mm, 1)
            pe.wait_ge(s_g_ready, 24)
            t_bank, f_bank, i_bank = banks[4], banks[6], banks[7]

            def hidden_group(u, g, ring):
                if g % 4 == 0:
                    pe.wait_ge(s_win_ready, 8 * u + g // 4 + 1)
                if g < 2 and positive(16 * u):
                    pe.wait_ge(s_q_copied, 16 * u)
                if positive(32 * u + g + 1 - ring):
                    pe.wait_ge(s_h_ready, 32 * u + g + 1 - ring)
                w = win[g // 4 % 2]
                for i in range(4):
                    first = (4 * (g % 4) + i) * WIN
                    mm = pe.matmul(banks[g % ring][:, 128 * i:128 * i + 128], w[:, first:first + 128], hidden_w,
                                   start=True, stop=True)
                mm.then_inc(s_hidden_mm, 1)

            def v_chunk(u, half, k, jr, every, between):
                chunk = 2 * k + jr
                if chunk == 1:
                    pe.wait_ge(s_y_ready, 8 * (u + 1))
                if chunk > 2:
                    pe.wait_ge(s_gated, 8 * u + chunk - 2)
                for s in range(2):
                    for tap in range(9):
                        dy, dx = tap // 3, tap % 3
                        row = 8 * (2 * s + jr) + dy
                        mm = pe.matmul(v_banks[chunk % 3][64 * s:64 * s + 64, :], v_w[:, 64 * tap:64 * tap + 64],
                                       at(xs[half], row * WP + 32 * k + dx, [32 * WP, 2], [WP, 8], [1, 32]),
                                       start=tap == 0, stop=tap == 8)
                        if (9 * s + tap) % every == every - 1:
                            between()
                mm.then_inc(s_v_mm, 1)

            def turn(u, k, jr):
                pe.wait_ge(s_y_norm, 8 * u + 2 * k + jr + 1)
                if k + jr > 0:
                    pe.wait_ge(s_t_copied, 8 * u + 2 * k + jr)
                for i in range(4):
                    tr = pe.transpose(t_bank[:, 128 * i:128 * i + 128],
                                      at(Y, 8 * k + 4 * jr + i, [32, 128]), ident)
                tr.then_inc(s_turned, 1)

            def project(u, k):
                if k > 0:
                    pe.wait_ge(s_res_done, 4 * u + k)
                for jr in range(2):
                    pe.wait_ge(s_gated, 8 * u + 2 * k + jr + 1)
                    mm = pe.matmul(f_bank[64 * jr:64 * jr + 64, :], small["w_out"], gated[jr], start=True, stop=True)
                mm.then_inc(s_project_mm, 1)

            def front(u, half, tail):
                groups = iter(range(32 if u is not None else 0))

                def hidden(n=1):
                    for g in islice(groups, n):
                        hidden_group(u, g, 4 if tail is None else 3)

                if tail is None:
                    hidden(32)
                    return
                v_half = 1 - half
                v_chunk(tail, v_half, 0, 0, 3, hidden)
                v_chunk(tail, v_half, 0, 1, 3, hidden)
                turn(tail, 0, 0)
                v_chunk(tail, v_half, 1, 0, 4, hidden)
                turn(tail, 0, 1)
                hidden(1)
                for k in range(1, 4):
                    v_chunk(tail, v_half, k, 1, 5, hidden)
                    project(tail, k - 1)
                    turn(tail, k, 0)
                    if k < 3:
                        v_chunk(tail, v_half, k + 1, 0, 5, hidden)
                    if k < 3 or u is None:
                        turn(tail, k, 1)

            def spectral(u, tail):
                def inverse(n):
                    pe.wait_ge(s_prod_ready, 16 * u + n + 1)
                    if n % 2 == 0:
                        if positive(8 * u + n // 2):
                            pe.wait_ge(s_y_ready, 8 * u + n // 2)
                    if n == 0 and tail is not None:
                        pe.wait_ge(s_gated, 8 * u)
                    for lam in range(2):
                        mm = pe.matmul(i_bank[64 * lam:64 * lam + 64, 256 * (n % 2):256 * (n % 2) + 256], small["inverse"],
                                       at(prod[n % 2], 64 * lam, [128, 4], [1, 64]), start=True, stop=True)
                    mm.then_inc(s_inverse_mm, 1)

                pe.wait_ge(s_h_ready, 32 * (u + 1))
                for n in range(16):
                    if positive(16 * u + n - 1):
                        pe.wait_ge(s_q_copied, 16 * u + n - 1)
                    for i in range(4):
                        ch = 4 * n + i
                        half = i % 2
                        mm = pe.matmul(banks[n % 2][64 * half:64 * half + 64, 128 * (i // 2):128 * (i // 2) + 128],
                                       G_q[:, 64 * ch:64 * ch + 64], hwin[:, 128 * ch:128 * ch + 128], start=True, stop=True)
                    mm.then_inc(s_q_mm, 1)
                    if n == 0 and tail is not None:
                        turn(tail, 3, 1)
                    if positive(16 * u + n - 1):
                        pe.wait_ge(s_prod_ready, 16 * u + n - 1)
                    for i in range(4):
                        ch = 4 * n + i
                        mm = pe.matmul(banks[2 + n % 2][:, 128 * i:128 * i + 128], G_k[0:WIN, 128 * ch:128 * ch + 128],
                                       hwin[0:WIN, 128 * (64 + ch):128 * (64 + ch) + 128], start=True, stop=True)
                    mm.then_inc(s_k_mm, 1)
                    if n == 1 and tail is not None:
                        project(tail, 3)
                    if n > 0:
                        inverse(n - 1)
                inverse(15)

            front(0, 0, None)
            spectral(0, None)
            with pe.Fori(0, NB - 1) as b:
                for half in (1, 0):
                    u = 2 * b + 2 - half
                    front(u, half, u - 1)
                    spectral(u, u - 1)
            front(LAST, 1, LAST - 1)
            spectral(LAST, LAST - 1)
            front(None, 0, LAST)
            project(LAST, 3)

        @block.scalar
        def _(act):
            act.wait_ge(s_qk_t, 1)
            act.activation(hidden_w, banks[6][:, 0:128], ACT.Copy).then_inc(s_hidden_hi, 1)
            act.activation(dw_t[0:9, :], banks[6][0:9, 128:256], ACT.Copy)
            act.wait_ge(s_v_t, 1)
            act.activation(v_w[:, 0:512], banks[7], ACT.Copy)
            act.activation(v_w[:, 512:576], banks[0][:, 0:64], ACT.Copy).then_inc(s_v_hi, 1)

            stats_psum = banks[4]

            def evacuate(here, k):
                b, n, s = here
                if k % 2 == 0 and positive(4 * (b - 2) + k // 2 + 1):
                    act.wait_ge(s_xl_ready, 4 * (b - 2) + k // 2 + 1)
                act.wait_ge(s_conv_mm, NCH * b + k + 1)
                act.activation(x2[s][:, 512 * k:512 * k + 512], banks[k % 4], ACT.Copy).then_inc(s_x2_ready, 1)

            SHIFTED_BY_ACT = {2: (3, 4), 3: (5, 6), 5: (7,)}

            def norm(prev, i):
                if prev is not None:
                    b, n, s = prev
                    act.wait_ge(s_shift2, b + 1)
                    act.wait_ge(s_x2_out[s], 64 * (n + 1))
                    piece = x2[s][:, QPIX // 2 * i:QPIX // 2 * (i + 1)]
                    act.activation(piece, piece, ACT.Identity, bias=tiny["shift2"], scale=tiny["scale2"]).then_inc(s_x2n_ready, 1)

            def high(prev, i):
                if prev is not None:
                    b, n, s = prev
                    rows = slice(16 * i, 16 * i + 16)
                    act.wait_ge(s_x2n_ready, 2 * b + 1 + i)
                    act.wait_ge(s_xn_out, 128 * b + 32)
                    act.activation(xh.rearrange("p (h w) -> p h w", w=WP)[:, rows, 1:W + 1],
                                   x2[s].rearrange("p (h w) -> p h w", w=W)[:, rows, :], ACT.Copy).then_inc(s_xh_ready, 1)

            def shift_right(after, i):
                if after is not None:
                    b, n, s = after
                    act.wait_ge(s_x3_mid_in[s], 16 * (n + 1))
                    dst, src = right_shift(s, i)
                    act.activation(dst, src, ACT.Copy).then_inc(s_right_act, 1)

            def slot(older, prev, here, after):
                for k in range(NCH):
                    if k == 4:
                        norm(prev, 0)
                        if after is not None:
                            act.wait_ge(s_pooled, after[0] + 1)
                            act.activation(tiny["gate_exp"], tiny["pooled"], ACT.Exp, scale=-1.0).then_inc(s_gate_exp, 1)
                        norm(prev, 1)
                    if k >= 6:
                        high(prev, k - 6)
                    for i in SHIFTED_BY_ACT.get(k, ()):
                        shift_right(after, i)
                    if k == 5 and after is not None:
                        act.wait_ge(s_neg_max_t, after[0] + 1)
                        act.activation(tiny["exps"][0:1, :], stats_psum[0:1, 4:8], ACT.Exp, scale=1.0 / TEMPERATURE,
                                       bias=tiny["neg_max_t"][0:1, :], accum_out=tiny["exp_sum"][0:1, :]).then_inc(s_exps, 1)
                    if here is not None:
                        evacuate(here, k)

            slots(act, slot)

            k_rows = G_k.rearrange("p (c m) -> p c m", m=128)
            q_rows = G_q.rearrange("p (c m) -> p c m", m=64)
            for i in range(24):
                act.wait_ge(s_g_mm, i + 1)
                dst = k_rows[:, :, 8 * i:8 * i + 8] if i < 16 else q_rows[:, :, 8 * i - 128:8 * i - 120]
                act.activation(dst, banks[i % 4].rearrange("p (m c) -> p c m", m=8), ACT.Copy).then_inc(s_g_ready, 1)
            act.wait_ge(s_hwin_zero, 1)

            h_rows = hwin.rearrange("p (c j) -> p c j", j=128)
            Y_out = Y.rearrange("p (s c j) -> p c s j", s=2, j=32)
            Y_sq = Y.rearrange("p (s c j) -> p s c j", s=2, j=32)

            def windows_out(u, g, ring):
                pr, k = g // 4, g % 4
                first = 64 * (pr // 4) + 32 * (pr // 2 % 2) + 8 * k + 4 * (pr % 2)
                act.wait_ge(s_hidden_mm, 32 * u + g + 1)
                act.activation(h_rows[0:WIN, :, first:first + 4],
                               banks[g % ring][0:WIN, :].rearrange("p (i c) -> p c i", i=4), ACT.Copy).then_inc(s_h_ready, 1)

            def square(u, p):
                act.wait_ge(s_y_centred, 8 * u + p + 1)
                if p > 1:
                    act.wait_ge(s_sq_sums, 8 * u + p - 1)
                act.activation(squares[:, 512 * (p % 2):512 * (p % 2) + 512].rearrange("p (s c j) -> p s c j", s=2, j=4),
                               Y_sq[:, :, :, 4 * p:4 * p + 4], ACT.Square).then_inc(s_squared, 1)

            def turned_out(u, k, jr):
                act.wait_ge(s_turned, 8 * u + 2 * k + jr + 1)
                if k > 0:
                    act.wait_ge(s_project_mm, 4 * u + k)
                for lam in range(2):
                    ins = act.activation(at(gated[jr], 256 * lam, [32, 8], [8, 4], [1, 8]),
                                         at(banks[4], 64 * lam, [8, 8], [128, 4], [1, 8]), ACT.Identity,
                                         bias=tiny["v_shift"], scale=tiny["v_scale"])
                ins.then_inc(s_t_copied, 1)

            def front(u, tail):
                groups = iter(range(32 if u is not None else 0))

                def some(n):
                    for g in islice(groups, n):
                        windows_out(u, g, 4 if tail is None else 3)

                if tail is None:
                    some(32)
                    return
                some(4)
                square(tail, 0)
                some(1)
                square(tail, 1)
                some(4)
                square(tail, 2)
                for p, groups_before in enumerate((3, 4, 4, 3, 3, 3, 3)):
                    some(groups_before)
                    turned_out(tail, p // 2, p % 2)
                    if p + 3 < 8:
                        square(tail, p + 3)
                if u is None:
                    turned_out(tail, 3, 1)

            def spectral(u, tail):
                if tail is not None:
                    turned_out(tail, 3, 1)
                for n in range(16):
                    if n % 2 == 1 and n >= 3:
                        inverse_out(u, n // 2 - 1)
                    act.wait_ge(s_q_mm, 16 * u + n + 1)
                    if positive(16 * u + n - 3):
                        act.wait_ge(s_prod_ready, 16 * u + n - 3)
                    for half in range(2):
                        src = banks[n % 2][64 * half:64 * half + 64, 0:256].rearrange("p (i j) -> p i j", i=2)
                        for to in range(2):
                            ins = act.activation(at(q_sb[n % 4][64 * to:64 * to + 64, :], 128 * half, [256, 2], [1, 128]), src, ACT.Copy)
                    ins.then_inc(s_q_copied, 1)
                inverse_out(u, 7)

            def inverse_out(u, e):
                act.wait_ge(s_inverse_mm, 16 * u + 2 * e + 2)
                act.activation(Y_out[:, 8 * e:8 * e + 8, :, :], banks[7].rearrange("p (c s j) -> p c s j", s=2, j=32),
                               ACT.Copy).then_inc(s_y_ready, 1)

            front(0, None)
            spectral(0, None)
            with act.Fori(0, NB - 1) as b:
                for half in (1, 0):
                    u = 2 * b + 2 - half
                    front(u, u - 1)
                    spectral(u, u - 1)
            front(LAST, LAST - 1)
            spectral(LAST, LAST - 1)
            front(None, LAST)

        @block.vector
        def _(dve):
            T = tiny
            dve.wait_ge(s_small_in, 16 * len(packs))
            dve.wait_ge(s_pads_zero, 2)
            dve.tensor_scalar(T["gammas"], small["gamma"], float(1 / np.sqrt(np.float32(1 + EPS))), None, ALU.mult).then_inc(s_prep, 1)
            dve.wait_ge(s_prep, 1)
            dve.tensor_reduce(T["qk_max"], small["hidden_qk"], X_AXIS, ALU.max, apply_absolute_value=True).then_inc(s_prep, 1)
            dve.wait_ge(s_prep, 2)
            dve.tensor_scalar(T["qk_max"], T["qk_max"], TINY, None, ALU.max).then_inc(s_prep, 1)
            dve.wait_ge(s_prep, 3)
            dve.reciprocal(T["qk_inv"], T["qk_max"]).then_inc(s_prep, 1)
            dve.wait_ge(s_prep, 4)
            dve.tensor_scalar(T["qk_back"], T["qk_max"], 1 / X_SCALE, None, ALU.mult).then_inc(s_prep, 1)
            dve.wait_ge(s_prep, 5)
            for g in range(4):
                dve.tensor_scalar(prep_qk[:, 32 * g:32 * g + 32], small["hidden_qk"], T["qk_inv"], None, ALU.mult).then_inc(s_prep, 1)
                dve.wait_ge(s_prep, 6 + g)
            dve.tensor_scalar(T["dw_qk_s"], small["dw_qk"], T["qk_back"], None, ALU.mult).then_inc(s_prep_qk, 1)
            dve.wait_ge(s_prep_qk, 1)
            dve.tensor_reduce(T["v_max"], small["hidden_v"], X_AXIS, ALU.max, apply_absolute_value=True).then_inc(s_prep, 1)
            dve.wait_ge(s_prep, 10)
            dve.tensor_scalar(T["v_max"], T["v_max"], TINY, None, ALU.max).then_inc(s_prep, 1)
            dve.wait_ge(s_prep, 11)
            dve.reciprocal(T["v_inv"], T["v_max"]).then_inc(s_prep, 1)
            dve.wait_ge(s_prep, 12)
            dve.tensor_reduce(T["d_max"], small["dw_v"], X_AXIS, ALU.max, apply_absolute_value=True).then_inc(s_prep, 1)
            dve.wait_ge(s_prep, 13)
            dve.tensor_scalar(T["d_max"], T["d_max"], TINY, None, ALU.max).then_inc(s_prep, 1)
            dve.wait_ge(s_prep, 14)
            dve.reciprocal(T["d_inv"], T["d_max"]).then_inc(s_prep, 1)
            dve.wait_ge(s_prep, 15)
            dve.tensor_scalar(T["dw_v_n"], small["dw_v"], T["d_inv"], None, ALU.mult).then_inc(s_prep, 1)
            dve.wait_ge(s_prep, 16)
            for tap in range(9):
                for g in range(4):
                    ins = dve.tensor_scalar(prep_v[:, 128 * tap + 32 * g:128 * tap + 32 * g + 32], small["hidden_v"],
                                            T["v_inv"], T["dw_v_n"][:, tap:tap + 1], ALU.mult, ALU.mult)
            ins.then_inc(s_prep_v, 1)
            dve.tensor_scalar(T["v_back"], T["v_max"], T["d_max"], 1 / X_SCALE, ALU.mult, ALU.mult).then_inc(s_prep, 1)
            dve.wait_ge(s_prep, 17)
            dve.tensor_scalar(T["v_scale"], small["norm_w"], T["v_back"], None, ALU.mult)
            dve.tensor_scalar(T["v_shift"], small["norm_b"], T["v_back"], None, ALU.mult)
            dve.wait_ge(s_hidden_hi, 1)
            dve.tensor_tensor(hidden_w[64:128, :], banks[6][64:128, 0:128], hidden_w[64:128, :], ALU.subtract)
            dve.wait_ge(s_v_hi, 1)
            dve.tensor_tensor(v_w[64:128, 0:512], banks[7][64:128, :], v_w[64:128, 0:512], ALU.subtract)
            dve.tensor_tensor(v_w[64:128, 512:576], banks[0][64:128, 0:64], v_w[64:128, 512:576], ALU.subtract).then_inc(s_low_parts, 1)

            stats_bank, corr_bank, norm_bank = banks[4], banks[5], banks[6]

            def aggregate(b, k, stats):
                dve.wait_ge(s_st[k], NCH * (b + 1))
                dve.memset(T[f"dev{k}"], 0.0)
                dve.bn_aggr(T[f"mv{k}"], stats).then_inc(s_mv[k], 1)

            def quarter_variance(b, k, bank):
                dve.wait_ge(s_mv[k], b + 1)
                dve.wait_ge(s_mean_mm[k], b + 1)
                dve.tensor_copy(T[f"mean{k}"], bank[:, 0:1])
                dve.tensor_tensor(T[f"dev{k}"], T[f"mv{k}"][:, 0:1], bank[:, 0:1], ALU.subtract).then_inc(s_dev[k], 1)
                dve.wait_ge(s_dev[k], b + 1)
                dve.scalar_tensor_tensor(T[f"varq{k}"], T[f"dev{k}"], T[f"dev{k}"], T[f"mv{k}"][:, 1:2], ALU.mult,
                                         ALU.add).then_inc(s_varq[k], 1)

            def variance_eps(b, k, bank):
                dve.wait_ge(s_var_mm[k], b + 1)
                dve.tensor_scalar(T[f"ve{k}"], bank[:, 1:2], EPS, None, ALU.add).then_inc(s_ve[k], 1)

            def first_stats(after, chunks):
                if after is not None:
                    b = after[0]
                    dve.wait_ge(s_xr_in, 64 * (b + 1))
                    for k in chunks:
                        dve.bn_stats(st1[:, 6 * k:6 * k + 6], xr[:, 512 * k:512 * k + 512]).then_inc(s_st[1], 1)

            def second_stats(here, k):
                if here is not None:
                    b, n, s = here
                    dve.wait_ge(s_x2_ready, NCH * b + k + 1)
                    dve.bn_stats(st2[:, 6 * k:6 * k + 6], x2[s][:, 512 * k:512 * k + 512]).then_inc(s_st[2], 1)

            def low(older, i):
                if older is not None:
                    b, n, s = older
                    dve.wait_ge(s_xh_ready, 2 * b + 1 + i // 2)
                    rows = slice(8 * i, 8 * i + 8)
                    padded = lambda a: a.rearrange("p (h w) -> p h w", w=WP)[:, rows, 1:W + 1]
                    dve.tensor_tensor(padded(xl), x2[s].rearrange("p (h w) -> p h w", w=W)[:, rows, :], padded(xh),
                                      ALU.subtract).then_inc(s_xl_ready, 1)

            def shift_right(after, i):
                if after is not None:
                    b, n, s = after
                    dve.wait_ge(s_x3_mid_in[s], 16 * (n + 1))
                    dst, src = right_shift(s, i)
                    dve.tensor_copy(dst, src).then_inc(s_right_dve, 1)

            def slot(older, prev, here, after):
                b0, b2 = prev and prev[0], after and after[0]
                for i in range(4):
                    low(older, i)
                second_stats(prev, NCH - 1)
                if prev is not None:
                    aggregate(b0, 2, st2)
                first_stats(after, range(NCH))
                if after is not None:
                    aggregate(b2, 1, st1)
                if prev is not None:
                    quarter_variance(b0, 2, norm_bank)
                second_stats(here, 0)
                if after is not None:
                    quarter_variance(b2, 1, stats_bank)
                if prev is not None:
                    variance_eps(b0, 2, norm_bank)
                second_stats(here, 1)
                if after is not None:
                    variance_eps(b2, 1, stats_bank)
                if prev is not None:
                    dve.wait_ge(s_rstd[2], b0 + 1)
                    dve.tensor_scalar(T["scale2"], T["rstd2"], X_SCALE, None, ALU.mult).then_inc(s_scale2, 1)
                    dve.wait_ge(s_scale2, b0 + 1)
                    dve.scalar_tensor_tensor(T["shift2"], T["mean2"], -1.0, T["scale2"], ALU.mult, ALU.mult).then_inc(s_shift2, 1)
                second_stats(here, 2)
                if after is not None:
                    dve.wait_ge(s_rstd[1], b2 + 1)
                    dve.scalar_tensor_tensor(T["shift1"], T["mean1"], -1.0, T["rstd1"], ALU.mult, ALU.mult).then_inc(s_shift1, 1)
                    dve.wait_ge(s_shift1, b2 + 1)
                    dve.scalar_tensor_tensor(T["quarter_xn"], T["mv1"][:, 0:1], T["rstd1"], T["shift1"], ALU.mult,
                                             ALU.add).then_inc(s_quarter_xn, 1)
                shift_right(after, 0)
                if here is None and prev is not None:
                    for i in range(2):
                        dve.wait_ge(s_taps_mm, i + 1)
                        dve.tensor_tensor(taps[i][0:96, :], taps_banks[i][0:96, :], row_mask[0:96, :], ALU.mult).then_inc(s_taps, 1)
                second_stats(here, 3)
                if after is not None:
                    dve.wait_ge(s_pooled_mm, b2 + 1)
                    dve.tensor_copy(T["pooled"], stats_bank[:, 2:3]).then_inc(s_pooled, 1)
                    dve.wait_ge(s_hid_mm, b2 + 1)
                    dve.tensor_scalar(T["hid"], stats_bank[:, 3:4], T["gammas"], small["beta"], ALU.mult, ALU.add).then_inc(s_hid, 1)
                    dve.wait_ge(s_hid, b2 + 1)
                    dve.tensor_scalar(T["hid_relu"], T["hid"], 0.0, None, ALU.max).then_inc(s_hid_relu, 1)
                if after is not None:
                    dve.wait_ge(s_logit_mm, b2 + 1)
                    dve.tensor_reduce(T["neg_max"][0:1, :], stats_bank[0:1, 4:8], X_AXIS, ALU.max, negate=True).then_inc(s_neg_max, 1)
                    dve.wait_ge(s_neg_max, b2 + 1)
                    dve.tensor_scalar(T["neg_max_t"][0:1, :], T["neg_max"][0:1, :], 1.0 / TEMPERATURE, None, ALU.mult).then_inc(s_neg_max_t, 1)
                second_stats(here, 4)
                if after is not None:
                    dve.wait_ge(s_gate_exp, b2 + 1)
                    dve.tensor_scalar(T["gate_den"], T["gate_exp"], 1.0, None, ALU.add).then_inc(s_gate_den, 1)
                    dve.wait_ge(s_gate_den, b2 + 1)
                    dve.reciprocal(T["gate"], T["gate_den"]).then_inc(s_gate, 1)
                    dve.wait_ge(s_gate, b2 + 1)
                    dve.tensor_scalar(T["chan_scale"], T["gate"], T["rstd1"], None, ALU.mult).then_inc(s_chan_scale, 1)
                    dve.wait_ge(s_exps, b2 + 1)
                    dve.reciprocal(T["exp_inv"][0:1, :], T["exp_sum"][0:1, :]).then_inc(s_exp_inv, 1)
                    dve.wait_ge(s_exp_inv, b2 + 1)
                    dve.tensor_scalar(T["att"][0:1, :], T["exps"][0:1, :], T["exp_inv"][0:1, :], None, ALU.mult).then_inc(s_att, 1)
                shift_right(after, 1)
                if after is not None:
                    weights(*after)
                second_stats(here, 5)
                if after is not None:
                    rows_and_edges(*after)
                shift_right(after, 2)
                second_stats(here, 6)

            def weights(b, n, s):
                dve.wait_ge(s_att_mm, b + 1)
                dve.tensor_copy(T["att_all"], stats_bank[:, 8:12]).then_inc(s_att_all, 1)
                dve.wait_ge(s_att_all, b + 1)
                agg, dyn = T["agg"][0:96, :], small["dyn_w"][0:96, :]
                dve.tensor_scalar(agg, dyn[:, 0:3], T["att_all"][0:96, 0:1], None, ALU.mult).then_inc(s_agg, 1)
                for k in range(1, 4):
                    dve.wait_ge(s_agg, 4 * b + k)
                    dve.scalar_tensor_tensor(agg, dyn[:, 3 * k:3 * k + 3], T["att_all"][0:96, k:k + 1], agg, ALU.mult,
                                             ALU.add).then_inc(s_agg, 1)
                dve.wait_ge(s_agg, 4 * b + 4)
                dve.wait_ge(s_chan_scale, b + 1)
                for dy in range(3):
                    dve.tensor_scalar(conv_w[s][0:96, 32 * dy:32 * dy + 32], small["conv1"][0:96, :], agg[:, dy:dy + 1],
                                      T["chan_scale"][0:96, :], ALU.mult, ALU.mult)
                dve.tensor_scalar(mean_w, small["tap_group"], T["mean1"], -1.0, ALU.mult, ALU.mult).then_inc(s_mean_w, 1)

            def rows_and_edges(b, n, s):
                dve.wait_ge(s_x3_left_in[s], 16 * (n + 1))
                dve.memset(at(x3[s][64:96, :], 2 * W - 1, [W, H]), 0.0).then_inc(s_edges, 1)
                dve.wait_ge(s_corr_mm, b + 1)
                middle = conv_w[s][32:64, 32:64]
                dve.tensor_tensor(middle, middle, ident[32:64, 32:64], ALU.add)
                dve.tensor_copy(conv_w[s][96:128, :], corr_bank[96:128, 0:96]).then_inc(s_conv_w, 1)

            slots(dve, slot)

            Y4 = Y.rearrange("p (s c j) -> p s c j", s=2, j=32)
            sq4 = [squares[:, 512 * i:512 * i + 512].rearrange("p (s c j) -> p s c j", s=2, j=4) for i in range(2)]
            by_chan = lambda a: a.rearrange("p s c j -> p s j c")
            over = lambda a: a.rearrange("p (s j) -> p s j", s=2).unsqueeze(2).broadcast_to([128, 2, 64, 4])
            pair = lambda a: a.rearrange("p (s j) -> p s j", s=2)

            def window(u, half, r, b=None):
                if positive(32 * u + 4 * (r - 1)):
                    dve.wait_ge(s_hidden_mm, 32 * u + 4 * (r - 1))
                if r == 0:
                    dve.wait_ge(s_xs_in[half], 64 * (b + 1))
                dve.tensor_copy(win[r % 2][:, 0:16 * WIN].rearrange("p (j y x) -> p j y x", y=10, x=10),
                                     at(xs[half], 8 * r * WP, [8, 16], [WP, 10], [1, 10])).then_inc(s_win_ready, 1)

            def channel_sums(u, i):
                dve.wait_ge(s_y_ready, 8 * u + 2 * i + 2)
                part = T["neg_mu"] if i == 0 else T["part_sums"]
                dve.tensor_reduce(pair(part), by_chan(Y4[:, :, 16 * i:16 * i + 16, :]), X_AXIS, ALU.add).then_inc(s_part_sums, 1)
                dve.wait_ge(s_part_sums, 4 * u + i + 1)
                if i > 0:
                    dve.tensor_tensor(T["neg_mu"], T["neg_mu"], T["part_sums"], ALU.add).then_inc(s_sums, 1)
                    dve.wait_ge(s_sums, 3 * u + i)

            def negative_mean(u):
                channel_sums(u, 3)
                dve.tensor_scalar(T["neg_mu"], T["neg_mu"], -1.0 / 64, None, ALU.mult).then_inc(s_neg_mu, 1)
                dve.wait_ge(s_neg_mu, u + 1)

            def centre(u, p):
                piece = Y4[:, :, :, 4 * p:4 * p + 4]
                neg_mu = pair(T["neg_mu"])[:, :, 4 * p:4 * p + 4].unsqueeze(2).broadcast_to([128, 2, 64, 4])
                dve.tensor_tensor(piece, piece, neg_mu, ALU.add).then_inc(s_y_centred, 1)

            def variance(u, p):
                dve.wait_ge(s_squared, 8 * u + p + 1)
                slot = slice(8 * (p % 2), 8 * (p % 2) + 8)
                dve.tensor_reduce(pair(T["sq_sums"][:, slot]), by_chan(sq4[p % 2]), X_AXIS, ALU.add).then_inc(s_sq_sums, 1)
                dve.wait_ge(s_sq_sums, 8 * u + p + 1)
                dve.tensor_scalar(T["var_eps"][:, slot], T["sq_sums"][:, slot], 1.0 / 64, EPS, ALU.mult, ALU.add).then_inc(s_var_eps, 1)

            def scale(u, p):
                piece = Y4[:, :, :, 4 * p:4 * p + 4]
                dve.wait_ge(s_root, 8 * u + p + 1)
                dve.wait_ge(s_y_centred, 8 * u + p + 1)
                slot = slice(8 * (p % 2), 8 * (p % 2) + 8)
                dve.tensor_tensor(piece, piece, over(T["rstd"][:, slot]), ALU.mult).then_inc(s_y_norm, 1)

            def gate(u, k, jr):
                dve.wait_ge(s_t_copied, 8 * u + 2 * k + jr + 1)
                dve.wait_ge(s_v_mm, 8 * u + 2 * k + jr + 1)
                dve.tensor_tensor(gated[jr], gated[jr], v_banks[(2 * k + jr) % 3], ALU.mult).then_inc(s_gated, 1)

            def residual(u, k):
                dve.wait_ge(s_project_mm, 4 * u + k + 1)
                if k == 0:
                    dve.wait_ge(s_res_in, 64 * (u + 1))
                piece = at(res, 32 * k, [1024, 2], [W, 8], [1, 32])
                dve.tensor_tensor(piece, banks[6].rearrange("p (l r w) -> p l r w", l=2, r=8), piece, ALU.add).then_inc(s_res_done, 1)

            def front(u, half, tail):
                rows = iter(range(2, 8) if u is not None else ())

                def windows(n=1):
                    for r in islice(rows, n):
                        window(u, half, r)

                if tail is None:
                    windows(6)
                    return
                negative_mean(tail)
                centre(tail, 0)
                centre(tail, 1)
                windows()
                variance(tail, 0)
                centre(tail, 2)
                windows()
                variance(tail, 1)
                scale(tail, 0)
                for p in range(8):
                    if p + 3 < 8:
                        centre(tail, p + 3)
                    if p + 2 < 8:
                        variance(tail, p + 2)
                    if p + 1 < 8:
                        scale(tail, p + 1)
                    if p in (0, 1, 2, 4):
                        windows()
                    if p < 7 or u is None:
                        gate(tail, p // 2, p % 2)
                    if p in (2, 4, 6):
                        residual(tail, p // 2 - 1)

            def spectral(u, tail, nxt):
                if tail is not None:
                    gate(tail, 3, 1)
                for n in range(16):
                    dve.wait_ge(s_q_copied, 16 * u + n + 1)
                    dve.wait_ge(s_k_mm, 16 * u + n + 1)
                    if positive(16 * u + n - 1):
                        dve.wait_ge(s_inverse_mm, 16 * u + n - 1)
                    dve.tensor_tensor(prod[n % 2], banks[2 + n % 2], q_sb[n % 4], ALU.mult).then_inc(s_prod_ready, 1)
                    if n == 1 and tail is not None:
                        residual(tail, 3)
                    if nxt is not None and n in (8, 11):
                        window(nxt[0], nxt[1], (n - 8) // 3, nxt[2])
                    if n in (5, 9, 13):
                        channel_sums(u, (n - 5) // 4)

            dve.wait_ge(s_win_room, 2)
            window(0, 0, 0, 0)
            window(0, 0, 1, 0)
            front(0, 0, None)
            spectral(0, None, (1, 1, 0))
            with dve.Fori(0, NB - 1) as b:
                for half in (1, 0):
                    u = 2 * b + 2 - half
                    front(u, half, u - 1)
                    spectral(u, u - 1, (u + 1, 1 - half, b + 1))
            front(LAST, 1, LAST - 1)
            spectral(LAST, LAST - 1, None)
            front(None, 0, LAST)
            residual(LAST, 3)


def kernel(**inputs):
    import concourse.bacc as bacc
    from concourse.bass_utils import run_bass_kernel_spmd

    a = {n: np.asarray(v) for n, v in inputs.items()}

    def padded(v, rows):
        return np.pad(v, ((0, rows - v.shape[0]), (0, 0)))

    def column(v):
        return v.reshape(-1, 1)

    hidden, dw = a["L1_conv_w_hidden"], a["L1_conv_w_dw"].reshape(192, 9)
    w_out = a["L1_conv_w_out"].T
    zero = np.zeros_like(w_out)
    dyn = a["L0_conv_weight"].reshape(4, 32, 3, 3)
    bias_row = np.zeros((96, 96), np.float32)
    bias_row[3, 32:64] = a["L0_conv_conv1_b"]
    arrays = {
        "x": a["x"],
        "w1": np.pad(a["L0_conv_att_w1"].T, ((0, 96), (0, 111))),
        "w2": padded(a["L0_conv_att_w2"].T, 128),
        "dyn_w": dyn.transpose(3, 1, 0, 2).reshape(96, 12),
        "conv1": np.tile(a["L0_conv_conv1_w"].T, (3, 1)),
        "bias_row": bias_row,
        "gamma": padded(column(a["L0_conv_bn_gamma"]), 128),
        "beta": padded(column(a["L0_conv_bn_beta"]), 128),
        "hidden_qk": hidden[0:128], "dw_qk": dw[0:128],
        "hidden_v": np.tile(hidden[128:], (2, 1)), "dw_v": np.tile(dw[128:], (2, 1)),
        "norm_w": np.tile(column(a["L1_conv_norm_w"]), (2, 1)), "norm_b": np.tile(column(a["L1_conv_norm_b"]), (2, 1)),
        "w_out": np.block([[w_out, zero], [zero, w_out]]),
        **constants(),
    }
    for pack, names in TABLES.items():
        arrays[pack] = np.concatenate([padded(arrays.pop(n), 128) for n, _ in names], axis=1)
    arrays = {n: np.ascontiguousarray(v) for n, v in arrays.items()}
    nc = bacc.Bacc("TRN2", target_bir_lowering=False, num_devices=1)
    t = {n: nc.dram_tensor(f"{n}_in", v.shape, mybir.dt.from_np(v.dtype), kind="ExternalInput").ap() for n, v in arrays.items()}
    out = nc.dram_tensor("out", a["x"].shape, mybir.dt.float32, kind="ExternalOutput").ap()
    build(nc, t, out)
    r = run_bass_kernel_spmd(nc, [{f"{n}_in": v for n, v in arrays.items()}], core_ids=[0])
    return r.results[0]["out"]
```
